# Optimizing a Trainium2 kernel written in Bass

```python
import numpy as np
import jax
import jax.numpy as jnp

def _softmax(x, axis=-1):
    return jax.nn.softmax(x, axis=axis)

def _gelu(x):
    return jax.nn.gelu(x, approximate=True)

def _silu(x):
    return jax.nn.silu(x)

def _sigmoid(x):
    return jax.nn.sigmoid(x)

def _layernorm(x, axis=-1, eps=1e-05):
    m = jnp.mean(x, axis=axis, keepdims=True)
    v = jnp.var(x, axis=axis, keepdims=True)
    return (x - m) / jnp.sqrt(v + eps)

def _scatter_add(tgt, idx, src, axis=0):
    return tgt.at[idx].add(src)

def _segment_sum(src, seg, n):
    return jax.ops.segment_sum(src, seg, n)
kernel_name = 'mk_cond_resid_d4_seqx_r4_9d0153'

def setup_inputs(seed: int=0):
    np.random.seed(seed)
    _w = jnp.asarray

    def _rec_inputs():
        import jax
        import jax.numpy as jnp
        _rk = jax.random.key(seed)
        x = -0.0003929 + 0.9999 * jax.random.normal(jax.random.fold_in(_rk, 1), (32, 64, 1024), jnp.float32)
        _lenS = 64 - jax.random.randint(jax.random.fold_in(_rk, 7), (32,), 0, max(1, 64 // 4) + 1, jnp.int32)
        _lenS2 = 64 - jax.random.randint(jax.random.fold_in(_rk, 8), (32,), 0, max(1, 64 // 4) + 1, jnp.int32)
        itok_B_78_3631 = jax.random.randint(jax.random.fold_in(_rk, 11), (32,), 78, 908, jnp.int32)
        itok_B_0_15 = jax.random.randint(jax.random.fold_in(_rk, 12), (32,), 0, 16, jnp.int32)
        itok_B_1_14 = jax.random.randint(jax.random.fold_in(_rk, 13), (32,), 1, 15, jnp.int32)
        itok_B_2_6 = jax.random.randint(jax.random.fold_in(_rk, 14), (32,), 2, 7, jnp.int32)
        return (x, itok_B_78_3631, itok_B_0_15, itok_B_1_14, itok_B_2_6)
    x, itok_B_78_3631, itok_B_0_15, itok_B_1_14, itok_B_2_6 = _rec_inputs()

    def _L0_cond_setup():
        import math
        import jax, jax.numpy as jnp
        import numpy as np
        B, H, N, L = (16, 64, 64, 1024)
        DT_MIN, DT_MAX = (0.001, 0.1)

        def _get_kernel(log_dt, C, log_A_real, A_imag, length):
            dt = jnp.exp(log_dt)
            Cc = C[..., 0] + 1j * C[..., 1]
            A = -jnp.exp(log_A_real) + 1j * A_imag
            dtA = A * dt[:, None]
            Ct = Cc * (jnp.exp(dtA) - 1.0) / A
            P = dtA[:, :, None] * jnp.arange(length, dtype=jnp.float32)
            K = 2.0 * jnp.einsum('hn,hnl->hl', Ct, jnp.exp(P)).real
            return K
        key = jax.random.key(seed)
        ks = jax.random.split(key, 5)
        u = jax.random.normal(ks[0], (B, H, L), dtype=jnp.float32)
        log_dt = jax.random.uniform(ks[1], (H,), dtype=jnp.float32) * (math.log(DT_MAX) - math.log(DT_MIN)) + math.log(DT_MIN)
        C = jax.random.normal(ks[2], (H, N, 2), dtype=jnp.float32)
        log_A_real = jnp.log(0.5 * jnp.ones((H, N), dtype=jnp.float32))
        A_imag = math.pi * jnp.broadcast_to(jnp.arange(N, dtype=jnp.float32), (H, N))
        D = jax.random.normal(ks[3], (H,), dtype=jnp.float32)
        length = jax.random.randint(ks[4], (B,), 1, L + 1, dtype=jnp.int32)
        return {'u': u, 'log_dt': log_dt, 'C': C, 'log_A_real': log_A_real, 'A_imag': A_imag, 'D': D, 'length': length}
    _L0_cond_all = _L0_cond_setup()
    _L0_cond_in = {k: v for k, v in _L0_cond_all.items() if k in ('log_dt', 'C', 'log_A_real', 'A_imag', 'D')}
    del _L0_cond_all

    def _L1_cond_setup():
        import jax, jax.numpy as jnp
        import numpy as np
        MAX_LORAS = 16
        IN, OUT = (1024, 1024)
        B, S = (8, 512)
        key = jax.random.key(seed)
        k1, k2, k3 = jax.random.split(key, 3)
        x = jax.random.normal(k1, (B, S, IN), dtype=jnp.float32)
        adapter_ids = jax.random.randint(k2, (B,), 0, MAX_LORAS)
        weight = jax.random.normal(k3, (MAX_LORAS, OUT, IN), dtype=jnp.float32) * 0.02
        return {'x': x, 'adapter_ids': adapter_ids, 'weight': weight}
    _L1_cond_all = _L1_cond_setup()
    _L1_cond_in = {k: v for k, v in _L1_cond_all.items() if k in ('weight',)}
    del _L1_cond_all

    def _L2_cond_setup():
        import jax, jax.numpy as jnp
        import numpy as np
        B, S, D_IN = (8, 512, 1024)
        A, D_OUT = (16, 1024)
        key = jax.random.key(seed)
        k1, k2, k3 = jax.random.split(key, 3)
        x = jax.random.normal(k1, (B, S, D_IN), dtype=jnp.float32)
        weight = jax.random.normal(k2, (A, D_OUT, D_IN), dtype=jnp.float32) * 0.02
        adapter_ids = jax.random.randint(k3, (B,), 0, A, dtype=jnp.int64)
        return {'x': x, 'weight': weight, 'adapter_ids': adapter_ids}
    _L2_cond_all = _L2_cond_setup()
    _L2_cond_in = {k: v for k, v in _L2_cond_all.items() if k in ('weight',)}
    del _L2_cond_all

    def _L3_cond_setup():
        import jax, jax.numpy as jnp
        import numpy as np
        B, N, H, F = (4, 128, 1024, 2752)
        L, R, RANK = (1, 16, 16)
        SCALE = 0.5
        key = jax.random.key(seed)
        ks = jax.random.split(key, 12)
        nrm = lambda k, shape, fan: jax.random.normal(k, shape, jnp.float32) * fan ** (-0.5)
        inp = {'x': jax.random.normal(ks[0], (B, N, H), jnp.float32), 'W_gate': nrm(ks[1], (F, H), H), 'W_up': nrm(ks[2], (F, H), H), 'W_down': nrm(ks[3], (H, F), F), 'A_gate': nrm(ks[4], (L, R, RANK, H), H), 'B_gate': nrm(ks[5], (L, R, F, RANK), RANK), 'A_up': nrm(ks[6], (L, R, RANK, H), H), 'B_up': nrm(ks[7], (L, R, F, RANK), RANK), 'A_down': nrm(ks[8], (L, R, RANK, F), F), 'B_down': nrm(ks[9], (L, R, H, RANK), RANK), 'lora_indices': jax.random.randint(ks[10], (B,), 0, R), 'layer_idx': 0}
        return inp
    _L3_cond_all = _L3_cond_setup()
    _L3_cond_in = {k: v for k, v in _L3_cond_all.items() if k in ('W_gate', 'W_up', 'W_down', 'A_gate', 'B_gate', 'A_up', 'B_up', 'A_down', 'B_down')}
    del _L3_cond_all
    return {'x': x, 'itok_B_78_3631': itok_B_78_3631, 'itok_B_0_15': itok_B_0_15, 'itok_B_1_14': itok_B_1_14, 'itok_B_2_6': itok_B_2_6, 'L0_cond_log_dt': _L0_cond_in['log_dt'], 'L0_cond_C': _L0_cond_in['C'], 'L0_cond_log_A_real': _L0_cond_in['log_A_real'], 'L0_cond_A_imag': _L0_cond_in['A_imag'], 'L0_cond_D': _L0_cond_in['D'], 'L1_cond_weight': _L1_cond_in['weight'], 'L2_cond_weight': _L2_cond_in['weight'], 'L3_cond_W_gate': _L3_cond_in['W_gate'], 'L3_cond_W_up': _L3_cond_in['W_up'], 'L3_cond_W_down': _L3_cond_in['W_down'], 'L3_cond_A_gate': _L3_cond_in['A_gate'], 'L3_cond_B_gate': _L3_cond_in['B_gate'], 'L3_cond_A_up': _L3_cond_in['A_up'], 'L3_cond_B_up': _L3_cond_in['B_up'], 'L3_cond_A_down': _L3_cond_in['A_down'], 'L3_cond_B_down': _L3_cond_in['B_down']}

def reference(x, itok_B_78_3631, itok_B_0_15, itok_B_1_14, itok_B_2_6, L0_cond_log_dt, L0_cond_C, L0_cond_log_A_real, L0_cond_A_imag, L0_cond_D, L1_cond_weight, L2_cond_weight, L3_cond_W_gate, L3_cond_W_up, L3_cond_W_down, L3_cond_A_gate, L3_cond_B_gate, L3_cond_A_up, L3_cond_B_up, L3_cond_A_down, L3_cond_B_down):
    import jax
    import jax.numpy as jnp

    def _L0_cond_ref(u, log_dt, C, log_A_real, A_imag, D, length):
        import math
        import jax, jax.numpy as jnp
        import numpy as np
        B, H, N, L = (16, 64, 64, 1024)
        DT_MIN, DT_MAX = (0.001, 0.1)

        def _get_kernel(log_dt, C, log_A_real, A_imag, length):
            dt = jnp.exp(log_dt)
            Cc = C[..., 0] + 1j * C[..., 1]
            A = -jnp.exp(log_A_real) + 1j * A_imag
            dtA = A * dt[:, None]
            Ct = Cc * (jnp.exp(dtA) - 1.0) / A
            P = dtA[:, :, None] * jnp.arange(length, dtype=jnp.float32)
            K = 2.0 * jnp.einsum('hn,hnl->hl', Ct, jnp.exp(P)).real
            return K
        Bq, Hq, Lq = u.shape
        K = _get_kernel(log_dt, C, log_A_real, A_imag, Lq)
        n = 2 * Lq
        kf = jnp.fft.rfft(K, n=n)
        uf = jnp.fft.rfft(u, n=n)
        y = jnp.fft.irfft(uf * kf[None], n=n)[..., :Lq]
        y = y + u * D[:, None]
        mask = (jnp.arange(Lq)[None, :] < length[:, None]).astype(u.dtype)
        return y * mask[:, None, :]

    def _L1_cond_ref(x, adapter_ids, weight):
        import jax, jax.numpy as jnp
        import numpy as np
        MAX_LORAS = 16
        IN, OUT = (1024, 1024)
        B, S = (8, 512)
        w = weight[adapter_ids]
        return jnp.einsum('bsi,boi->bso', x, w)

    def _L2_cond_ref(x, weight, adapter_ids):
        import jax, jax.numpy as jnp
        import numpy as np
        B, S, D_IN = (8, 512, 1024)
        A, D_OUT = (16, 1024)
        w = weight[adapter_ids]
        return jnp.einsum('bij,bkj->bik', x, w)

    def _L3_cond_ref(x, W_gate, W_up, W_down, A_gate, B_gate, A_up, B_up, A_down, B_down, lora_indices, layer_idx):
        import jax, jax.numpy as jnp
        import numpy as np
        B, N, H, F = (4, 128, 1024, 2752)
        L, R, RANK = (1, 16, 16)
        SCALE = 0.5

        def lora_add(base, inp, A, B):
            Ab = A[layer_idx][lora_indices]
            Bb = B[layer_idx][lora_indices]
            t = jnp.einsum('bri,bni->bnr', Ab, inp)
            return base + jnp.einsum('bor,bnr->bno', Bb, t) * SCALE
        gate = lora_add(jnp.einsum('bnh,fh->bnf', x, W_gate), x, A_gate, B_gate)
        up = lora_add(jnp.einsum('bnh,fh->bnf', x, W_up), x, A_up, B_up)
        act = jax.nn.silu(gate) * up
        down = lora_add(jnp.einsum('bnf,hf->bnh', act, W_down), act, A_down, B_down)
        return down
    x = x + _L0_cond_ref(x, L0_cond_log_dt, L0_cond_C, L0_cond_log_A_real, L0_cond_A_imag, L0_cond_D, itok_B_78_3631)
    x = x + _L1_cond_ref(x, itok_B_0_15, L1_cond_weight)
    x = x + _L2_cond_ref(x, L2_cond_weight, itok_B_1_14)
    x = x + _L3_cond_ref(x, L3_cond_W_gate, L3_cond_W_up, L3_cond_W_down, L3_cond_A_gate, L3_cond_B_gate, L3_cond_A_up, L3_cond_B_up, L3_cond_A_down, L3_cond_B_down, itok_B_2_6, 0)
    return x

_drawn_inputs = setup_inputs


def setup_inputs(seed=0):
    import zlib

    import numpy as np

    out = dict(_drawn_inputs(seed))
    spreads = {'L0_cond_log_A_real': (-0.6931471824645996, 0.2)}
    factors = {}
    for name, (base, spread) in spreads.items():
        noise = np.random.default_rng([zlib.crc32(name.encode()), seed]).standard_normal(out[name].shape)
        drawn = base * np.exp(spread * noise) if base else spread * noise
        out[name] = jnp.asarray(drawn.astype(out[name].dtype))
    for name, factor in factors.items():
        out[name] = (out[name] * factor).astype(out[name].dtype)
    return out
```

```python
import math
from contextlib import ExitStack

import concourse.bass as bass
from concourse import mybir

F32 = mybir.dt.float32
F32R = mybir.dt.float32r
I32 = mybir.dt.int32
ALU = mybir.AluOpType
ACT = mybir.ActivationFunctionType

P = 128
B, H, L = 32, 64, 1024
LT = L // P
ROWS = B * H
NS = 64
KB = 32
KPAD = P + L

CH = 16
NCHUNK = H // CH
TG = 4
UG = 8

WC = 4
WCO = L // WC

FF = 2752
FT = -(-FF // P)
F0 = 12
F1 = FT - F0
TILE = 512
NTILE = ROWS // TILE
TB = TILE // H
R = 16
NPAN = 2 + 2 * F0 + 1 + LT + 2 * F1 + 1 + LT
RAW = 4
PANB = 12
AD0 = 2 + 2 * F0
GU1 = AD0 + 1 + LT
AD1 = GU1 + 2 * F1
GATE = (0, 2)
DOWN = (4, 5, 7)
BANK_A, BANK_AD = 7, 6
CHUNK_LINKS = 13
assert NPAN % RAW == 0 and F0 % 2 == 0 and F1 % 2 == 0

PI = float.fromhex("0x1.921fb4p+1")
TWO_PI = 2 * math.pi
TWO_PI_1 = 6.28125
TWO_PI_2 = round((TWO_PI - TWO_PI_1) * 2 ** 19) / 2 ** 19
TWO_PI_3 = TWO_PI - TWO_PI_1 - TWO_PI_2
LN2_1 = 0.693359375
LN2_2 = math.log(2) - LN2_1
MAGIC = 1.5 * 2 ** 23


def build(nc, ins, out):
    with ExitStack() as ctx:
        sem = lambda name: ctx.enter_context(nc.semaphore(name))

        def sb(stack, name, shape, dt=F32):
            return stack.enter_context(nc.sbuf_tensor(name, shape, dt))

        kpad = nc.dram_tensor("kpad", [H, KPAD], F32).ap()
        lora_a = nc.dram_tensor("picked_a", [NTILE, 2, P, TB, LT * R], F32).ap()
        lora_ad = nc.dram_tensor("picked_ad", [NTILE, P, TB, FT * R], F32).ap()
        lora_b = nc.dram_tensor("picked_b", [NTILE, 2 * FT, P, P], F32).ap()
        lora_bd = nc.dram_tensor("picked_bd", [NTILE, LT, P, P], F32).ap()

        X = sb(ctx, "X", [P, LT, ROWS])
        ids = sb(ctx, "ids", [1, 3 * B], I32)
        lora_mask = sb(ctx, "lora_mask", [P, TB, H])
        tick = sb(ctx, "tick", [1, 8])

        with ExitStack() as s:
            toep = sb(s, "toep", [P, 2, TG, L])
            u = sb(s, "u", [P, 2, UG, LT, B])
            urev = sb(s, "urev", [P, 2, UG, LT, B])
            par = sb(s, "par", [P, 5, H])
            drow = sb(s, "drow", [1, H])
            leni = sb(s, "leni", [P, B], I32)
            lenf = sb(s, "lenf", [P, B])
            lpos = sb(s, "lpos", [P, LT])
            lmask = sb(s, "lmask", [P, LT, B])
            kk = sb(s, "kk", [P, 2 * KB])
            quarter = sb(s, "quarter", [P, 4])
            ex = sb(s, "ex", [P, 12, H])
            exi = sb(s, "exi", [P, 2, H], I32)
            dta = sb(s, "dta", [P, 2, H])
            ct = sb(s, "ct", [P, 2, H])
            ang = sb(s, "ang", [P, CH, 2 * KB])
            turn = sb(s, "turn", [P, CH, 2 * KB])
            mag = sb(s, "mag", [P, CH, 2 * KB])
            red = sb(s, "red", [P, CH, 2 * KB])
            red2 = sb(s, "red2", [P, CH, KB])
            sin1 = sb(s, "sin1", [P, CH, 2 * KB])
            sin2 = sb(s, "sin2", [P, CH, KB])
            ge = sb(s, "ge", [P, CH, 2 * KB])
            ksb = sb(s, "ksb", [KB, CH, KB])
            zrow = sb(s, "zrow", [H, P])
            masked = sb(s, "masked", [P, 2, 2, LT, B])

        with ExitStack() as s:
            W = sb(s, "W", [P, 2 * WC, LT, WCO])

        with ExitStack() as s:
            xh = sb(s, "xh", [P, LT, TILE], F32R)
            xl = sb(s, "xl", [P, LT, TILE], F32R)
            acth = sb(s, "acth", [P, F0, TILE], F32R)
            actl = sb(s, "actl", [P, F0, TILE], F32R)
            raw = sb(s, "raw", [P, RAW, PANB * P])
            ph = sb(s, "ph", [P, 2, PANB * P], F32R)
            pl = sb(s, "pl", [P, 2, PANB * P], F32R)
            tmh = sb(s, "tmh", [P, 2, TILE], F32R)
            tml = sb(s, "tml", [P, 2, TILE], F32R)
            hid = sb(s, "hid", [P, 2, TILE])

        ps = ctx.enter_context(nc.psum_tensor("ps", [P, 8, 512], F32))

        par_in = sem("par_in")
        ids_in = sem("ids_in")
        consts = sem("consts")
        zero_set = sem("zero_set")
        zero_out = sem("zero_out")
        dve_link = sem("dve_link")
        half_arg = sem("half_arg")
        half_sin = sem("half_sin")
        u_in = [sem(f"u_in{i}") for i in range(2)]
        toep_in = [sem(f"toep_in{i}") for i in range(2)]
        mag_arg = sem("mag_arg")
        exp_done = sem("exp_done")
        sin_arg = sem("sin_arg")
        sin_done = sem("sin_done")
        ge_ready = sem("ge_ready")
        kmm_done = sem("kmm_done")
        k_copied = sem("k_copied")
        k_ready = sem("k_ready")
        k_out = sem("k_out")
        conv_done = sem("conv_done")
        conv_free = sem("conv_free")
        x1_done = sem("x1_done")
        w_in = [sem(f"w_in{i}") for i in range(2 * WC)]
        w_used = sem("w_used")
        x_added = sem("x_added")
        lora_out = sem("lora_out")
        raw_in = [sem(f"raw_in{i}") for i in range(RAW)]
        hi_ready = sem("hi_ready")
        lo_ready = sem("lo_ready")
        panel_done = sem("panel_done")
        xh_ready = sem("xh_ready")
        xl_ready = sem("xl_ready")
        th_ready = sem("th_ready")
        t_ready = sem("t_ready")
        sig_ready = sem("sig_ready")
        silu_ready = sem("silu_ready")
        hid_ready = sem("hid_ready")
        act_ready = sem("act_ready")
        d_added = sem("d_added")
        y_out = sem("y_out")

        block = ctx.enter_context(nc.Block())
        PAIRS = H // 2
        CONVB = 4
        KBANK = 6

        def bank(i):
            return ps[:, i, :]

        @block.sync
        def _(sp):
            sp.dma_start(par[:], ins["params"]).then_inc(par_in, 16)
            sp.dma_start(drow[:], ins["D"]).then_inc(par_in, 16)
            sp.dma_start(leni[:], ins["length"].to_broadcast([P, B])).then_inc(par_in, 16)
            sp.dma_start(ids[:], ins["ids"]).then_inc(ids_in, 16)
            sp.wait_ge(zero_set, 1)
            sp.dma_start(kpad[:, 0:P], zrow[:]).then_inc(zero_out, 16)

            def load_inputs(g, i):
                sp.dma_start(u[:, i], ins["u"][:, bass.ds(g * UG, UG)]).then_inc(u_in[i], 16)
                sp.dma_start(urev[:, i], ins["urev"][:, bass.ds(g * UG, UG)]).then_inc(u_in[i], 16)

            def load_toeplitz(g, i):
                base = kpad[bass.ds(g * TG, TG), 1:1 + L]
                dims = [[1, P], [KPAD, TG], [1, L]]
                src = bass.AP(tensor=base.tensor, offset=base.offset, ap=dims)
                sp.dma_start(toep[:, i], src).then_inc(toep_in[i], 16)

            load_inputs(0, 0)
            load_inputs(1, 1)
            sp.wait_ge(zero_out, 16)
            for i in range(2):
                sp.wait_ge(k_out, 16)
                load_toeplitz(i, i)
            with sp.Fori(0, NCHUNK - 1) as c:
                for i in range(2):
                    sp.wait_ge(conv_done, c * (CH // 2) + (i + 1) * (TG // 2))
                    load_toeplitz(c * 4 + 2 + i, i)
                for i in range(2):
                    sp.wait_ge(x1_done, c * (CH // 2) + (i + 1) * (UG // 2))
                    load_inputs(c * 2 + 2 + i, i)
                    sp.wait_ge(conv_done, c * (CH // 2) + (i + 3) * (TG // 2))
                    if i == 0:
                        sp.wait_ge(k_out, c * 16 + 32)
                    load_toeplitz(c * 4 + 4 + i, i)
            for i in range(2):
                sp.wait_ge(conv_done, (NCHUNK - 1) * (CH // 2) + (i + 1) * (TG // 2))
                load_toeplitz(4 * NCHUNK - 2 + i, i)

            sp.wait_ge(ids_in, 16)
            for layer, w in enumerate((ins["w1"], ins["w2"])):
                with sp.Fori(0, B // 2) as it:
                    for half in range(2):
                        pick = sp.value_load(ids[0:1, bass.ds(it * 2 + (layer * B + half), 1)],
                                             min_val=0, max_val=15)
                        for c in range(WC):
                            slot = half * WC + c
                            sp.wait_ge(w_used, it * (2 * WC) + (layer * B * WC + slot + 1))
                            src = w[bass.ds(pick, 1), c].rearrange("a p i o -> (a p) i o")
                            sp.dma_start(W[:, slot], src).then_inc(w_in[slot], 16)

            def load(n, count, src, at=0, incs=32):
                width = src.shape[-1]
                sp.dma_start(raw[:, n % RAW, at:at + width], src).then_inc(raw_in[n % RAW], incs)

            def room(count):
                sp.wait_ge(lo_ready, count + 1)

            def load_adapter(n, count, t, k):
                room(count)
                load(n, count, lora_a[bass.ds(t, 1), k].rearrange("t p b w -> (t p) (b w)"))

            def load_down_adapter(n, t, first, tiles):
                room(t * NPAN + n)
                sp.dma_start(raw[:, n % RAW, 0:TB * tiles * R].rearrange("p (b w) -> p b w", b=TB),
                             lora_ad[bass.ds(t, 1), :, :, first * R:(first + tiles) * R]
                             .rearrange("t p b w -> (t p) b w")).then_inc(raw_in[n % RAW], 32)

            def load_gate_up(n, t, j, pan):
                room(t * NPAN + j * 4 + n)
                load(n, 0, ins["wgu"][bass.ds(pan, 1)].rearrange("a p w -> (a p) w"), incs=16)
                load(n, 0, lora_b[bass.ds(t, 1), bass.ds(pan, 1)].rearrange("t a p w -> (t a p) w"),
                     at=LT * P, incs=16)

            sp.wait_ge(lora_out, NTILE * TB * 16 * 5)
            load_adapter(0, 0, 0, 0)
            load_adapter(1, 1, 0, 1)
            with sp.Fori(0, NTILE) as t:
                for k in range(2):
                    load_gate_up(2 + k, t, 0, k)
                with sp.Fori(0, F0 // 2 - 1) as j:
                    for k in range(4):
                        load_gate_up(4 + k, t, j, j * 4 + (2 + k))
                for k in range(2):
                    load_gate_up(AD0 - 2 + k, t, 0, 2 * F0 - 2 + k)
                load_down_adapter(AD0, t, 0, F0)
                for o in range(LT):
                    room(t * NPAN + (AD0 + 1 + o))
                    load(AD0 + 1 + o, 0, ins["wd0"][o])
                for k in range(2):
                    load_gate_up(GU1 + k, t, 0, 2 * F0 + k)
                with sp.Fori(0, F1 // 2 - 1) as j:
                    for k in range(4):
                        load_gate_up(GU1 + 2 + k, t, j, j * 4 + (2 * F0 + 2 + k))
                for k in range(2):
                    load_gate_up(AD1 - 2 + k, t, 0, 2 * FT - 2 + k)
                load_down_adapter(AD1, t, F0, F1)
                for o in range(LT):
                    room(t * NPAN + (AD1 + 1 + o))
                    load(AD1 + 1 + o, 0, ins["wd1"][o], incs=16)
                    load(AD1 + 1 + o, 0, lora_bd[bass.ds(t, 1), o].rearrange("t p w -> (t p) w"),
                         at=F1 * P, incs=16)
                for k in range(2):
                    load_adapter(NPAN + k, t * NPAN + (NPAN + k), (t + 1) % NTILE, k)

        @block.gpsimd
        def _(pool):
            pool.memset(zrow[:], 0.0).then_inc(zero_set, 1)
            pool.iota(kk[:, 0:KB], pattern=[[1, KB]], base=0, channel_multiplier=0,
                      allow_small_or_imprecise_dtypes=True).then_inc(consts, 1)
            pool.iota(kk[:, KB:2 * KB], pattern=[[KB, KB]], base=0, channel_multiplier=0,
                      allow_small_or_imprecise_dtypes=True).then_inc(consts, 1)
            pool.iota(lpos[:], pattern=[[P, LT]], base=0, channel_multiplier=1,
                      allow_small_or_imprecise_dtypes=True).then_inc(consts, 1)
            for i, (upper, lower) in enumerate(((0.25, 0.0), (math.pi / 2, 0.0), (2.0, -2.0))):
                pool.wait_ge(consts, 3 + 2 * i)
                pool.memset(quarter[0:NS, i:i + 1], upper).then_inc(consts, 1)
                pool.wait_ge(consts, 4 + 2 * i)
                pool.memset(quarter[NS:P, i:i + 1], lower).then_inc(consts, 1)
            pool.wait_ge(consts, 9)
            pool.memset(lora_mask[:], 0.5).then_inc(consts, 1)
            pool.wait_ge(consts, 10)
            pool.affine_select(out=lora_mask[:], in_=lora_mask[:], compare_op=ALU.is_ge, fill=0.0, base=0,
                               pattern=[[-R, TB], [0, H]], channel_multiplier=1).then_inc(consts, 1)
            pool.wait_ge(consts, 11)
            pool.affine_select(out=lora_mask[:], in_=lora_mask[:], compare_op=ALU.is_ge, fill=0.0, base=R - 1,
                               pattern=[[R, TB], [0, H]], channel_multiplier=-1).then_inc(consts, 1)

            pool.wait_ge(ids_in, 16)
            with pool.Fori(0, NTILE) as t:
                for b in range(TB):
                    pick = pool.value_load(ids[0:1, bass.ds(t * TB + (2 * B + b), 1)], min_val=0, max_val=15)
                    one, tile = bass.ds(pick, 1), bass.ds(t, 1)
                    for k in range(2):
                        pool.dma_start(lora_a[tile, k, :, b].rearrange("t p w -> (t p) w"),
                                       ins["lora_a"][one, k].rearrange("a p w -> (a p) w")).then_inc(lora_out, 16)
                    pool.dma_start(lora_ad[tile, :, b].rearrange("t p w -> (t p) w"),
                                   ins["lora_ad"][one].rearrange("a p w -> (a p) w")).then_inc(lora_out, 16)
                    pool.dma_start(lora_b[tile, :, b * R:(b + 1) * R].rearrange("t a r w -> (t a) (r w)"),
                                   ins["lora_b"][one].rearrange("a n r w -> (a n) (r w)")).then_inc(lora_out, 16)
                    pool.dma_start(lora_bd[tile, :, b * R:(b + 1) * R].rearrange("t a r w -> (t a) (r w)"),
                                   ins["lora_bd"][one].rearrange("a n r w -> (a n) (r w)")).then_inc(lora_out, 16)

            with pool.Fori(0, NTILE) as t:
                pool.wait_ge(d_added, t * (2 * LT) + 2 * LT)
                pool.dma_start(out[bass.ds(t, 1)].rearrange("t p l w -> (t p) l w"),
                               X[:, :, bass.ds(t * TILE, TILE)]).then_inc(y_out, 16)
            pool.wait_ge(y_out, 16 * NTILE)

        @block.scalar
        def _(act):
            act.wait_ge(half_arg, 1)
            nc.scalar.activation(ex[:, 8:10], ex[:, 8:10], ACT.Sin).then_inc(half_sin, 1)

            def sines(c):
                act.wait_ge(mag_arg, c + 1)
                nc.scalar.activation(mag[:], mag[:], ACT.Exp).then_inc(exp_done, 1)
                act.wait_ge(sin_arg, c + 1)
                nc.scalar.activation(sin1[:], red[:], ACT.Sin).then_inc(sin_done, 1)
                nc.scalar.activation(sin2[:], red2[:], ACT.Sin).then_inc(sin_done, 1)

            def kernel_out(c):
                act.wait_ge(kmm_done, c + 1)
                if not isinstance(c, int) or c > 0:
                    act.wait_ge(k_out, c * 16)
                nc.scalar.activation(ksb[:], ps[0:KB, KBANK, :].rearrange("a (c b) -> a c b", c=CH),
                                     ACT.Copy).then_inc(k_copied, 1)
                act.wait_ge(k_ready, c + 1)
                dst = kpad[bass.ds(c * CH, CH), P:KPAD].rearrange("c (a b) -> a c b", a=KB)
                act.dma_start(dst, ksb[:]).then_inc(k_out, 16)

            sines(0)
            kernel_out(0)
            with act.Fori(1, NCHUNK) as c:
                sines(c)
                kernel_out(c)

            def come(n, t, j=0):
                act.wait_ge(raw_in[n % RAW], (t * (NPAN // RAW) + j + (n // RAW + 1)) * 32)
                act.wait_ge(panel_done, t * NPAN + j * 4 + (n + 1))

            def cut(n, blocks, t, j=0):
                come(n, t, j)
                nc.scalar.activation(ph[:, n % 2, 0:blocks * P], raw[:, n % RAW, 0:blocks * P],
                                     ACT.Copy).then_inc(hi_ready, 1)

            def cut_adapter(n, blocks, t):
                come(n, t)
                nc.scalar.activation(
                    ph[:, n % 2, 0:blocks * P].rearrange("p (k b r) -> p b k r", b=TB, r=R),
                    raw[:, n % RAW, 0:blocks * P].rearrange("p (b k r) -> p b k r", b=TB, r=R),
                    ACT.Copy).then_inc(hi_ready, 1)

            def cut_rows(t):
                nc.scalar.activation(xh[:], X[:, :, bass.ds(t * TILE, TILE)], ACT.Copy).then_inc(xh_ready, 1)

            def sigmoid(pair, n, t, j=0):
                act.wait_ge(panel_done, t * NPAN + j * 4 + (n + 3))
                nc.scalar.activation(hid[:, pair % 2], bank(GATE[pair % 2]),
                                     ACT.Sigmoid).then_inc(sig_ready, 1)

            cut_adapter(0, LT, 0)
            cut_adapter(1, LT, 0)
            act.wait_ge(x_added, 2 * B + 2)
            cut_rows(0)
            with act.Fori(0, NTILE) as t:
                cut(2, LT + 1, t)
                cut(3, LT + 1, t)
                with act.Fori(0, F0 // 2 - 1) as j:
                    for k in range(2):
                        cut(4 + 2 * k, LT + 1, t, j)
                        cut(5 + 2 * k, LT + 1, t, j)
                        sigmoid(k, 3 + 2 * k, t, j)
                cut(AD0 - 2, LT + 1, t)
                cut(AD0 - 1, LT + 1, t)
                sigmoid(F0 - 2, AD0 - 3, t)
                cut_adapter(AD0, F0, t)
                cut(AD0 + 1, F0, t)
                sigmoid(F0 - 1, AD0 - 1, t)
                for o in range(1, LT):
                    cut(AD0 + 1 + o, F0, t)
                cut(GU1, LT + 1, t)
                cut(GU1 + 1, LT + 1, t)
                with act.Fori(0, F1 // 2 - 1) as j:
                    for k in range(2):
                        cut(GU1 + 2 + 2 * k, LT + 1, t, j)
                        cut(GU1 + 3 + 2 * k, LT + 1, t, j)
                        sigmoid(F0 + k, GU1 + 1 + 2 * k, t, j)
                cut(AD1 - 2, LT + 1, t)
                cut(AD1 - 1, LT + 1, t)
                sigmoid(FT - 2, AD1 - 3, t)
                cut_adapter(AD1, F1, t)
                cut(AD1 + 1, F1 + 1, t)
                sigmoid(FT - 1, AD1 - 1, t)
                cut(AD1 + 2, F1 + 1, t)
                cut_rows((t + 1) % NTILE)
                for o in range(2, LT):
                    cut(AD1 + 1 + o, F1 + 1, t)
                for k in range(2):
                    cut_adapter(NPAN + k, LT, t)

        @block.vector
        def _(dve):
            V = nc.vector
            linked = [0]

            def link(ins, before=0):
                linked[0] += 1
                ins.then_inc(dve_link, 1)
                dve.wait_ge(dve_link, before + linked[0])

            def round_turns(t, before=0):
                link(V.tensor_scalar_add(t, t, MAGIC), before)
                link(V.tensor_scalar_add(t, t, -MAGIC), before)

            def expm1_of(x, n, r, q, two):
                link(V.tensor_scalar(n, x, 1 / math.log(2), None, ALU.mult))
                round_turns(n)
                link(V.tensor_scalar(n, n, -126.0, 127.0, ALU.max, ALU.min))
                link(V.scalar_tensor_tensor(out=r, in0=n, scalar=-LN2_1, in1=x, op0=ALU.mult, op1=ALU.add))
                link(V.scalar_tensor_tensor(out=r, in0=n, scalar=-LN2_2, in1=r, op0=ALU.mult, op1=ALU.add))
                link(V.tensor_scalar(q, r, 1 / 40320, None, ALU.mult))
                for d in (5040, 720, 120, 24, 6, 2, 1):
                    link(V.scalar_tensor_tensor(out=q, in0=q, scalar=1 / d, in1=r, op0=ALU.add, op1=ALU.mult))
                link(V.tensor_scalar(two, n, 127.0, float(2 ** 23), ALU.add, ALU.mult))

            def tt(out_, a, b, op, before=0):
                link(V.tensor_tensor(out=out_, in0=a, in1=b, op=op), before)

            V.memset(tick[:, 0:1], 0.0).then_inc(conv_free, CONVB)
            link(V.memset(ex[:], 0.0))
            dve.wait_ge(par_in, 48)
            dve.wait_ge(consts, 12)

            two = exi[:, 0:2].bitcast(F32)
            expm1_of(par[:, 0:2], ex[:, 0:2], ex[:, 2:4], ex[:, 4:6], exi[:, 0:2])
            tt(ex[:, 6:8], ex[:, 4:6], two, ALU.mult)
            tt(ex[:, 6:8], ex[:, 6:8], two, ALU.add)
            link(V.tensor_scalar(ex[:, 6], ex[:, 6], -1.0, None, ALU.mult))
            ar, dt, ai = ex[:, 6], ex[:, 7], par[:, 2]
            tt(dta[:, 0], ar, dt, ALU.mult)
            tt(dta[:, 1], ai, dt, ALU.mult)
            expm1_of(dta[:, 0], ex[:, 0], ex[:, 1], ex[:, 2], exi[:, 0])
            one = exi[:, 0].bitcast(F32)
            tt(ex[:, 2], ex[:, 2], one, ALU.mult)
            link(V.scalar_tensor_tensor(out=ex[:, 3], in0=one, scalar=-1.0, in1=ex[:, 2],
                                        op0=ALU.add, op1=ALU.add))
            link(V.tensor_scalar(ex[:, 10], dta[:, 1], 0.5, None, ALU.mult))
            link(V.tensor_scalar(ex[:, 11], dta[:, 1], 0.5, None, ALU.mult))
            link(V.tensor_scalar(ex[:, 4:6], ex[:, 10:12], 1 / TWO_PI, None, ALU.mult))
            link(V.tensor_scalar_add(ex[:, 5], ex[:, 5], 0.25))
            round_turns(ex[:, 4:6])
            for i, part in enumerate((TWO_PI_1, TWO_PI_2, TWO_PI_3)):
                link(V.scalar_tensor_tensor(out=ex[:, 8:10], in0=ex[:, 4:6], scalar=-part,
                                            in1=ex[:, 10:12] if i == 0 else ex[:, 8:10],
                                            op0=ALU.mult, op1=ALU.add))
            link(V.tensor_scalar_add(ex[:, 9], ex[:, 9], math.pi / 2))
            V.tensor_scalar(ex[:, 8:10], ex[:, 8:10], PI, -PI, ALU.min, ALU.max).then_inc(half_arg, 1)
            dve.wait_ge(half_sin, 1)
            em, s2, c2, cr, ci = ex[:, 3], ex[:, 8], ex[:, 9], par[:, 3], par[:, 4]
            link(V.tensor_scalar_add(ex[:, 0], em, 1.0))
            link(V.scalar_tensor_tensor(out=ex[:, 0], in0=ex[:, 0], scalar=-2.0, in1=s2,
                                        op0=ALU.mult, op1=ALU.mult))
            tt(ex[:, 1], ex[:, 0], s2, ALU.mult)
            tt(ex[:, 1], ex[:, 1], em, ALU.add)
            tt(ex[:, 2], ex[:, 0], c2, ALU.mult)
            tt(ex[:, 4], cr, ex[:, 1], ALU.mult)
            tt(ex[:, 5], ci, ex[:, 2], ALU.mult)
            tt(ex[:, 4], ex[:, 4], ex[:, 5], ALU.add)
            tt(ex[:, 5], ci, ex[:, 1], ALU.mult)
            tt(ex[:, 8], cr, ex[:, 2], ALU.mult)
            tt(ex[:, 5], ex[:, 5], ex[:, 8], ALU.subtract)
            tt(ex[:, 8], ar, ar, ALU.mult)
            tt(ex[:, 9], ai, ai, ALU.mult)
            tt(ex[:, 8], ex[:, 8], ex[:, 9], ALU.add)
            link(V.reciprocal(ex[:, 8], ex[:, 8]))
            link(V.tensor_scalar(ex[:, 8], ex[:, 8], quarter[:, 2:3], None, ALU.mult))
            for o, a, b, op in ((0, ex[:, 4], ex[:, 5], ALU.add), (1, ex[:, 5], ex[:, 4], ALU.subtract)):
                tt(ex[:, 9], a, ar, ALU.mult)
                tt(ex[:, 10], b, ai, ALU.mult)
                tt(ex[:, 9], ex[:, 9], ex[:, 10], op)
                tt(ct[:, o], ex[:, 9], ex[:, 8], ALU.mult)
            link(V.tensor_copy(lenf[:], leni[:]))
            tt(lmask[:], lenf[:].unsqueeze(1).to_broadcast([P, LT, B]),
               lpos[:].unsqueeze(2).to_broadcast([P, LT, B]), ALU.is_gt)

            def over_k(a, c, n):
                return a[:, bass.ds(c * CH, CH)].unsqueeze(2).to_broadcast([P, CH, n])

            all_k = kk[:].unsqueeze(1).to_broadcast([P, CH, 2 * KB])

            def phases(c, before=0):
                V.tensor_tensor(out=mag[:], in0=over_k(dta[:, 0], c, 2 * KB), in1=all_k,
                                op=ALU.mult).then_inc(mag_arg, 1)
                tt(ang[:], over_k(dta[:, 1], c, 2 * KB), all_k, ALU.mult, before)
                link(V.tensor_scalar(turn[:], ang[:], 1 / TWO_PI, quarter[:, 0:1], ALU.mult, ALU.add), before)
                round_turns(turn[:], before)
                for i, part in enumerate((TWO_PI_1, TWO_PI_2, TWO_PI_3)):
                    link(V.scalar_tensor_tensor(out=red[:], in0=turn[:], scalar=-part,
                                                in1=ang[:] if i == 0 else red[:],
                                                op0=ALU.mult, op1=ALU.add), before)

            def quarter_turns(c, before=0):
                link(V.tensor_scalar(red[:], red[:], quarter[:, 1:2], PI, ALU.add, ALU.min), before)
                link(V.tensor_scalar(red[:], red[:], -PI, None, ALU.max), before)
                r = red[:, :, KB:2 * KB]
                link(V.tensor_scalar(turn[:, :, 0:KB], r, PI / 2, -TWO_PI, ALU.is_gt, ALU.mult), before)
                link(V.scalar_tensor_tensor(out=red2[:], in0=r, scalar=PI / 2, in1=turn[:, :, 0:KB],
                                            op0=ALU.add, op1=ALU.add), before)
                V.tensor_scalar(red2[:], red2[:], PI, -PI, ALU.min, ALU.max).then_inc(sin_arg, 1)

            def powers(c, before=0):
                dve.wait_ge(exp_done, c + 1)
                dve.wait_ge(sin_done, c * 2 + 2)
                if not isinstance(c, int):
                    dve.wait_ge(kmm_done, c)
                V.tensor_tensor(out=ge[:, :, 0:KB], in0=sin1[:, :, 0:KB], in1=mag[:, :, 0:KB], op=ALU.mult)
                V.tensor_tensor(out=sin1[:, :, KB:2 * KB], in0=sin1[:, :, KB:2 * KB],
                                in1=mag[:, :, KB:2 * KB], op=ALU.mult)
                tt(sin2[:], sin2[:], mag[:, :, KB:2 * KB], ALU.mult, before)
                V.tensor_tensor(out=sin1[:, :, KB:2 * KB], in0=sin1[:, :, KB:2 * KB],
                                in1=over_k(ct[:, 0], c, KB), op=ALU.mult)
                tt(sin2[:], sin2[:], over_k(ct[:, 1], c, KB), ALU.mult, before)
                V.tensor_tensor(out=ge[:, :, KB:2 * KB], in0=sin1[:, :, KB:2 * KB], in1=sin2[:],
                                op=ALU.add).then_inc(ge_ready, 1)

            def add_d(c):
                dve.wait_ge(k_copied, c + 1)
                V.tensor_tensor(out=ksb[0:1, :, 0:1], in0=ksb[0:1, :, 0:1],
                                in1=drow[0:1, bass.ds(c * CH, CH)].unsqueeze(2), op=ALU.add).then_inc(k_ready, 1)

            def add_conv(c, i):
                q = c * (CH // 2) + i
                dve.wait_ge(conv_done, q + 1)
                mi = masked[:, i % 2].rearrange("p e l b -> p e (l b)")
                V.tensor_tensor(out=mi, in0=bank(i % CONVB).rearrange("p (e w) -> p e w", e=2),
                                in1=lmask[:].rearrange("p l b -> p (l b)").unsqueeze(1)
                                .to_broadcast([P, 2, LT * B]), op=ALU.mult).then_inc(conv_free, 1)
                dve.wait_ge(conv_free, q + (CONVB + 1))
                chan = 2 * (i % (UG // 2))
                V.tensor_tensor(out=X[:].rearrange("p l (b h) -> p h l b", h=H)[:, bass.ds(c * CH + 2 * i, 2)],
                                in0=masked[:, i % 2], in1=u[:, i // (UG // 2), chan:chan + 2],
                                op=ALU.add).then_inc(x1_done, 1)

            phases(0)
            quarter_turns(0)
            powers(0)
            add_d(0)
            setup_links = linked[0]
            with dve.Fori(0, NCHUNK - 1) as c:
                linked[0] = setup_links
                before = c * CHUNK_LINKS
                add_conv(c, 0)
                phases(c + 1, before)
                add_conv(c, 1)
                add_conv(c, 2)
                quarter_turns(c + 1, before)
                add_conv(c, 3)
                powers(c + 1, before)
                add_conv(c, 4)
                add_conv(c, 5)
                add_d(c + 1)
                add_conv(c, 6)
                add_conv(c, 7)
                assert linked[0] - setup_links == CHUNK_LINKS
            for i in range(CH // 2):
                add_conv(NCHUNK - 1, i)

            dve.wait_ge(x1_done, PAIRS)
            V.memset(tick[:, 1:2], 0.0).then_inc(w_used, 2 * WC)
            V.memset(tick[:, 2:3], 0.0).then_inc(x_added, 2)
            V.memset(tick[:, 3:4], 0.0).then_inc(lo_ready, RAW)
            V.memset(tick[:, 4:5], 0.0).then_inc(panel_done, 2)

            with dve.Fori(0, B) as it:
                for half in range(2):
                    dve.wait_ge(w_used, it * (2 * WC) + (half + 1) * WC + 2 * WC)
                    rows = X[:, :, bass.ds((it * 2 + half) % B * H, H)]
                    V.tensor_tensor(out=rows, in0=bank(half).rearrange("p (l h) -> p l h", h=H), in1=rows,
                                    op=ALU.add).then_inc(x_added, 1)

            def cut(n, blocks, t, j=0):
                dve.wait_ge(hi_ready, t * NPAN + j * 4 + (n + 1))
                V.tensor_tensor(out=pl[:, n % 2, 0:blocks * P], in0=raw[:, n % RAW, 0:blocks * P],
                                in1=ph[:, n % 2, 0:blocks * P].bitcast(F32),
                                op=ALU.subtract).then_inc(lo_ready, 1)

            def cut_adapter(n, blocks, t):
                dve.wait_ge(hi_ready, t * NPAN + (n + 1))
                way = dict(b=TB, r=R)
                V.tensor_tensor(
                    out=pl[:, n % 2, 0:blocks * P].rearrange("p (k b r) -> p b k r", **way),
                    in0=raw[:, n % RAW, 0:blocks * P].rearrange("p (b k r) -> p b k r", **way),
                    in1=ph[:, n % 2, 0:blocks * P].bitcast(F32).rearrange("p (k b r) -> p b k r", **way),
                    op=ALU.subtract).then_inc(lo_ready, 1)

            def cut_rows(t, count):
                dve.wait_ge(xh_ready, count)
                V.tensor_tensor(out=xl[:], in0=X[:, :, bass.ds(t * TILE, TILE)], in1=xh[:].bitcast(F32),
                                op=ALU.subtract).then_inc(xl_ready, 1)

            def adapter(k, count, n, bk, t):
                dve.wait_ge(panel_done, t * NPAN + (n + 3))
                mask, prod, part = lora_mask[:].rearrange("p b h -> p (b h)"), bank(bk), hid[:, count % 2]
                V.tensor_tensor(out=part, in0=prod, in1=mask, op=ALU.mult)
                V.tensor_tensor(out=tmh[:, k], in0=prod, in1=mask, op=ALU.mult).then_inc(th_ready, 1)
                dve.wait_ge(th_ready, t * 3 + (count + 1))
                V.tensor_tensor(out=tml[:, k], in0=part, in1=tmh[:, k].bitcast(F32),
                                op=ALU.subtract).then_inc(t_ready, 1)

            def hidden(pair, at, n, t, j=0):
                count, two_ = t * FT + j * 2 + (pair + 1), pair % 2
                dve.wait_ge(panel_done, t * NPAN + j * 4 + (n + 3))
                dve.wait_ge(sig_ready, count)
                V.tensor_tensor(out=hid[:, two_], in0=hid[:, two_], in1=bank(GATE[two_]),
                                op=ALU.mult).then_inc(silu_ready, 1)
                dve.wait_ge(silu_ready, count)
                one = bass.ds(j * 2 + at, 1) if not isinstance(j, int) else slice(at, at + 1)
                hi, lo = acth[:, one].rearrange("p a w -> p (a w)"), actl[:, one].rearrange("p a w -> p (a w)")
                V.tensor_tensor(out=hi, in0=hid[:, two_], in1=bank(GATE[two_] + 1), op=ALU.mult)
                V.tensor_tensor(out=hid[:, two_], in0=hid[:, two_], in1=bank(GATE[two_] + 1),
                                op=ALU.mult).then_inc(hid_ready, 1)
                dve.wait_ge(hid_ready, count)
                V.tensor_tensor(out=lo, in0=hid[:, two_], in1=hi.bitcast(F32),
                                op=ALU.subtract).then_inc(act_ready, 1)

            def down(o, n, t):
                dve.wait_ge(panel_done, t * NPAN + (n + 3))
                rows = X[:, o, bass.ds(t * TILE, TILE)]
                V.tensor_tensor(out=rows, in0=bank(DOWN[o % 3]), in1=rows, op=ALU.add).then_inc(d_added, 1)

            cut_adapter(0, LT, 0)
            cut_adapter(1, LT, 0)
            cut_rows(0, 1)
            with dve.Fori(0, NTILE) as t:
                cut(2, LT + 1, t)
                adapter(0, 0, 0, BANK_A, t)
                cut(3, LT + 1, t)
                adapter(1, 1, 1, BANK_AD, t)
                with dve.Fori(0, F0 // 2 - 1) as j:
                    for k in range(2):
                        cut(4 + 2 * k, LT + 1, t, j)
                        cut(5 + 2 * k, LT + 1, t, j)
                        hidden(k, k, 3 + 2 * k, t, j)
                cut(AD0 - 2, LT + 1, t)
                cut(AD0 - 1, LT + 1, t)
                hidden(F0 - 2, F0 - 2, AD0 - 3, t)
                cut_adapter(AD0, F0, t)
                cut(AD0 + 1, F0, t)
                hidden(F0 - 1, F0 - 1, AD0 - 1, t)
                cut(AD0 + 2, F0, t)
                for o in range(2, LT):
                    cut(AD0 + 1 + o, F0, t)
                    down(o - 2, AD0 - 1 + o, t)
                cut(GU1, LT + 1, t)
                down(LT - 2, GU1 - 2, t)
                cut(GU1 + 1, LT + 1, t)
                down(LT - 1, GU1 - 1, t)
                with dve.Fori(0, F1 // 2 - 1) as j:
                    for k in range(2):
                        cut(GU1 + 2 + 2 * k, LT + 1, t, j)
                        cut(GU1 + 3 + 2 * k, LT + 1, t, j)
                        hidden(F0 + k, k, GU1 + 1 + 2 * k, t, j)
                cut(AD1 - 2, LT + 1, t)
                cut(AD1 - 1, LT + 1, t)
                hidden(FT - 2, F1 - 2, AD1 - 3, t)
                cut_adapter(AD1, F1, t)
                cut(AD1 + 1, F1 + 1, t)
                hidden(FT - 1, F1 - 1, AD1 - 1, t)
                cut(AD1 + 2, F1 + 1, t)
                adapter(0, 2, AD1, BANK_AD, t)
                cut_rows((t + 1) % NTILE, t + 2)
                for o in range(2, LT):
                    cut(AD1 + 1 + o, F1 + 1, t)
                    down(o - 2, AD1 - 1 + o, t)
                for k in range(2):
                    cut_adapter(NPAN + k, LT, t)
                    down(LT - 2 + k, NPAN - 2 + k, t)

        @block.tensor
        def _(pe):
            mm = nc.tensor.matmul

            def kernels(c):
                pe.wait_ge(ge_ready, c + 1)
                if not isinstance(c, int):
                    pe.wait_ge(k_copied, c)
                for h in range(CH):
                    last = mm(ps[0:KB, KBANK, h * KB:(h + 1) * KB], lhsT=ge[:, h, KB:2 * KB],
                              rhs=ge[:, h, 0:KB], start=True, stop=True)
                last.then_inc(kmm_done, 1)

            def convolve(c, g):
                half = g // 2
                pe.wait_ge(toep_in[g % 2], (c * 2 + (half + 1)) * 16)
                pe.wait_ge(u_in[half], (c + 1) * 32)
                for i in range(2):
                    pair = 2 * g + i
                    pe.wait_ge(conv_free, c * (CH // 2) + (pair + 1))
                    for e in range(2):
                        tile = toep[:, g % 2, 2 * i + e]
                        rows = urev[:, half, (pair % 4) * 2 + e].rearrange("p l b -> p (l b)")
                        for d in range(LT):
                            n = (LT - d) * B
                            last = mm(ps[:, pair % CONVB, (e + 1) * LT * B - n:(e + 1) * LT * B],
                                      lhsT=tile[:, d * P:(d + 1) * P], rhs=rows[:, 0:n],
                                      start=d == 0, stop=d == LT - 1)
                    last.then_inc(conv_done, 1)

            kernels(0)
            with pe.Fori(0, NCHUNK - 1) as c:
                convolve(c, 0)
                convolve(c, 1)
                convolve(c, 2)
                kernels(c + 1)
                convolve(c, 3)
            for g in range(4):
                convolve(NCHUNK - 1, g)

            with pe.Fori(0, B) as it:
                for half in range(2):
                    pe.wait_ge(x_added, it * 2 + (half + 1))
                    seq = (it * 2 + half) % B * H
                    for c in range(WC):
                        slot = half * WC + c
                        pe.wait_ge(w_in[slot], it * 16 + 16)
                        for o in range(WCO // P):
                            at = (c * (WCO // P) + o) * H
                            for k in range(LT):
                                last = mm(ps[:, half, at:at + H], lhsT=W[:, slot, k, o * P:(o + 1) * P],
                                          rhs=X[:, k, bass.ds(seq, H)], start=k == 0, stop=k == LT - 1)
                        last.then_inc(w_used, 1)

            def panel(n, bk, blocks, hi, lo, t, j=0, start=True, stop=True, extra=None, ready=None):
                pe.wait_ge(lo_ready, t * NPAN + j * 4 + (n + RAW + 1))
                moving = [(hi[:, k], lo[:, k]) for k in range(blocks)] + ([extra[0]] if extra else [])
                for k, (mh, ml) in enumerate(moving):
                    if extra and k == blocks:
                        pe.wait_ge(*extra[1])
                    if ready and k in ready:
                        pe.wait_ge(act_ready, ready[k])
                    wh, wl = ph[:, n % 2, k * P:(k + 1) * P], pl[:, n % 2, k * P:(k + 1) * P]
                    first, end = start and k == 0, stop and k == len(moving) - 1
                    mm(bank(bk), lhsT=wh, rhs=mh, start=first, stop=False)
                    mm(bank(bk), lhsT=wh, rhs=ml, start=False, stop=False)
                    last = mm(bank(bk), lhsT=wl, rhs=mh, start=False, stop=end)
                last.then_inc(panel_done, 1)

            def gate_up(pair, n, t, j=0):
                for k in range(2):
                    panel(n + k, GATE[pair % 2] + k, LT, xh, xl, t, j,
                          extra=((tmh[:, k], tml[:, k]), (t_ready, t * 3 + (k + 1))))

            with pe.Fori(0, NTILE) as t:
                pe.wait_ge(xl_ready, t + 1)
                panel(0, BANK_A, LT, xh, xl, t)
                panel(1, BANK_AD, LT, xh, xl, t)
                with pe.Fori(0, F0 // 2) as j:
                    for k in range(2):
                        gate_up(k, 2 + 2 * k, t, j)
                done = lambda k: t * FT + (k + 1)
                panel(AD0, BANK_AD, F0, acth, actl, t, stop=False,
                      ready={0: done(F0 - 3), F0 - 2: done(F0 - 2), F0 - 1: done(F0 - 1)})
                for o in range(LT):
                    panel(AD0 + 1 + o, DOWN[o % 3], F0, acth, actl, t)
                with pe.Fori(0, F1 // 2) as j:
                    for k in range(2):
                        gate_up(k, GU1 + 2 * k, t, j)
                panel(AD1, BANK_AD, F1, acth, actl, t, start=False,
                      ready={0: done(FT - 3), F1 - 2: done(FT - 2), F1 - 1: done(FT - 1)})
                for o in range(LT):
                    panel(AD1 + 1 + o, DOWN[o % 3], F1, acth, actl, t,
                          extra=((tmh[:, 0], tml[:, 0]), (t_ready, t * 3 + 3)))


def kernel(**inputs):
    import numpy as np
    import concourse.bacc as bacc
    from concourse.bass_utils import run_bass_kernel_spmd

    f = {k.replace("_cond", ""): np.asarray(v) for k, v in inputs.items()}

    x = f["x"].reshape(B, H, LT, P)
    u = x.transpose(3, 1, 2, 0)
    state = [f["L0_log_A_real"].T, np.broadcast_to(f["L0_log_dt"][None, :], (NS, H)), f["L0_A_imag"].T,
             f["L0_C"][:, :, 0].T, f["L0_C"][:, :, 1].T]
    params = np.stack(state, axis=1)
    picked = lambda w: w.reshape(16, WC, WCO, LT, P).transpose(0, 1, 4, 3, 2)
    pad = FT * P - FF
    tiles = lambda w: np.pad(w, ((0, pad), (0, 0))).reshape(FT, P, LT, P).transpose(0, 3, 2, 1)
    wgu = np.stack([tiles(f["L3_W_gate"]), tiles(f["L3_W_up"])], axis=1).reshape(2 * FT, P, LT * P)
    wd = np.pad(f["L3_W_down"], ((0, 0), (0, pad))).reshape(LT, P, FT, P).transpose(0, 3, 2, 1)
    la = lambda a: a[0].reshape(16, R, LT, P).transpose(0, 3, 2, 1).reshape(16, P, LT * R)
    lad = np.pad(f["L3_A_down"][0], ((0, 0), (0, 0), (0, pad))).reshape(16, R, FT, P)
    lb = lambda b: np.pad(b[0], ((0, 0), (0, pad), (0, 0))).reshape(16, FT, P, R).transpose(0, 1, 3, 2)
    arrays = {
        "u": u,
        "urev": u[::-1],
        "params": np.concatenate([params, params]),
        "D": f["L0_D"].reshape(1, H),
        "length": f["itok_B_78_3631"].reshape(1, B),
        "ids": np.concatenate([f["itok_B_0_15"], f["itok_B_1_14"], f["itok_B_2_6"]]).reshape(1, 3 * B),
        "w1": picked(f["L1_weight"]),
        "w2": picked(f["L2_weight"]),
        "wgu": wgu,
        "wd0": wd[:, :, :F0].reshape(LT, P, F0 * P),
        "wd1": wd[:, :, F0:].reshape(LT, P, F1 * P),
        "lora_a": np.stack([la(f["L3_A_gate"]), la(f["L3_A_up"])], axis=1),
        "lora_ad": lad.transpose(0, 3, 2, 1).reshape(16, P, FT * R),
        "lora_b": np.stack([lb(f["L3_B_gate"]), lb(f["L3_B_up"])], axis=2).reshape(16, 2 * FT, R, P),
        "lora_bd": f["L3_B_down"][0].reshape(16, LT, P, R).transpose(0, 1, 3, 2),
    }
    arrays = {k: np.ascontiguousarray(v) for k, v in arrays.items()}
    nc = bacc.Bacc("TRN2", target_bir_lowering=False, num_devices=1)
    ins = {k: nc.dram_tensor("in_" + k, v.shape, mybir.dt.from_np(v.dtype), kind="ExternalInput").ap()
           for k, v in arrays.items()}
    out = nc.dram_tensor("y", [NTILE, P, LT, TILE], F32, kind="ExternalOutput").ap()
    build(nc, ins, out)
    run = run_bass_kernel_spmd(nc, [{"in_" + k: v for k, v in arrays.items()}], core_ids=[0])
    y = run.results[0]["y"]
    return np.ascontiguousarray(y.transpose(0, 3, 2, 1).reshape(B, H, L))
```

```python
import math
from contextlib import ExitStack

import concourse.bass as bass
from concourse import mybir

F32 = mybir.dt.float32
F32R = mybir.dt.float32r
I32 = mybir.dt.int32
ALU = mybir.AluOpType
ACT = mybir.ActivationFunctionType

P = 128
B, H, L = 32, 64, 1024
LT = L // P
ROWS = B * H
NS = 64
KB = 32
KPAD = P + L

CH = 16
NCHUNK = H // CH
TG = 4
UG = 8

WC = 4
WK = LT // 2
WN = L // 2
NPICK = 16
STEPS = (B + NPICK) // 2
SPARE = 3
ROOM = STEPS + 2
assert STEPS % 2 == 0 and ROOM <= B

FF = 2752
FT = -(-FF // P)
F0 = 12
F1 = FT - F0
TILE = 512
NTILE = ROWS // TILE
TB = TILE // H
R = 16
NPAN = 2 + 2 * F0 + 1 + LT + 2 * F1 + 1 + LT
RAW = 4
PANB = 12
AD0 = 2 + 2 * F0
GU1 = AD0 + 1 + LT
AD1 = GU1 + 2 * F1
GATE = (0, 2)
DOWN = (4, 5, 7)
BANK_A, BANK_AD = 7, 6
TURN = 4
CHUNK_LINKS = 13
assert NPAN % RAW == 0 and F0 % 2 == 0 and F1 % 2 == 0

PI = float.fromhex("0x1.921fb4p+1")
TWO_PI = 2 * math.pi
TWO_PI_1 = 6.28125
TWO_PI_2 = round((TWO_PI - TWO_PI_1) * 2 ** 19) / 2 ** 19
TWO_PI_3 = TWO_PI - TWO_PI_1 - TWO_PI_2
LN2_1 = 0.693359375
LN2_2 = math.log(2) - LN2_1
MAGIC = 1.5 * 2 ** 23


def build(nc, ins, out):
    with ExitStack() as ctx:
        sem = lambda name: ctx.enter_context(nc.semaphore(name))

        def sb(stack, name, shape, dt=F32):
            return stack.enter_context(nc.sbuf_tensor(name, shape, dt))

        kpad = nc.dram_tensor("kpad", [H, KPAD], F32).ap()
        lora_a = nc.dram_tensor("picked_a", [NTILE, 2, P, TB, LT * R], F32).ap()
        lora_ad = nc.dram_tensor("picked_ad", [NTILE, P, TB, FT * R], F32).ap()
        lora_b = nc.dram_tensor("picked_b", [NTILE, 2 * FT, P, P], F32).ap()
        lora_bd = nc.dram_tensor("picked_bd", [NTILE, LT, P, P], F32).ap()

        X = sb(ctx, "X", [P, B + SPARE, LT, H])
        hid = [X[:, B + k].rearrange("p l h -> p (l h)") for k in range(2)]
        lora_mask = X[:, B + 2].rearrange("p l h -> p (l h)").rearrange("p (b h) -> p b h", h=H)

        early = ExitStack()
        ids = sb(early, "ids", [1, 3 * B], I32)
        table = sb(early, "table", [2, 3, ROOM], I32)
        turns = sb(early, "turns", [2, 1], I32)
        tick = sb(early, "tick", [1, 8])

        with ExitStack() as s:
            toep = sb(s, "toep", [P, 2, TG, L])
            u = sb(s, "u", [P, 2, UG, LT, B])
            urev = sb(s, "urev", [P, 2, UG, LT, B])
            par = sb(s, "par", [P, 5, H])
            drow = sb(s, "drow", [1, H])
            leni = sb(s, "leni", [P, B], I32)
            lenf = sb(s, "lenf", [P, B])
            lpos = sb(s, "lpos", [P, LT])
            lmask = sb(s, "lmask", [P, LT, B])
            kk = sb(s, "kk", [P, 2 * KB])
            quarter = sb(s, "quarter", [P, 4])
            ex = sb(s, "ex", [P, 12, H])
            exi = sb(s, "exi", [P, 2, H], I32)
            dta = sb(s, "dta", [P, 2, H])
            ct = sb(s, "ct", [P, 2, H])
            ang = sb(s, "ang", [P, CH, 2 * KB])
            turn = sb(s, "turn", [P, CH, 2 * KB])
            mag = sb(s, "mag", [P, CH, 2 * KB])
            red = sb(s, "red", [P, CH, 2 * KB])
            red2 = sb(s, "red2", [P, CH, KB])
            sin1 = sb(s, "sin1", [P, CH, 2 * KB])
            sin2 = sb(s, "sin2", [P, CH, KB])
            ge = sb(s, "ge", [P, CH, 2 * KB])
            ksb = sb(s, "ksb", [KB, CH, KB])
            zrow = sb(s, "zrow", [H, P])
            masked = sb(s, "masked", [P, 2, 2, LT, B])
            picki = sb(s, "picki", [2, B], I32)
            tri = sb(s, "tri", [2, B, B])
            seqs = sb(s, "seqs", [2, B])
            steps = sb(s, "steps", [2, ROOM])
            spare = sb(s, "spare", [2, 2, ROOM])
            pk = sb(s, "pk", [2, 6, B])
            pair = sb(s, "pair", [2, B, B])
            hit = sb(s, "hit", [2, 2, ROOM, B])
            found = sb(s, "found", [2, 5, ROOM])

        with ExitStack() as s:
            W = sb(s, "W", [P, WC, WK, WN])
            wh = sb(s, "wh", [P, WC, WK, WN], F32R)
            wl = sb(s, "wl", [P, WC, WK, WN], F32R)
            rh = sb(s, "rh", [P, 2, LT, 2 * H], F32R)
            rl = sb(s, "rl", [P, 2, LT, 2 * H], F32R)
            prod = sb(s, "prod", [2 * H, 2, L])
            ident = sb(s, "ident", [P, P])
        early.close()

        with ExitStack() as s:
            xh = sb(s, "xh", [P, LT, TILE], F32R)
            xl = sb(s, "xl", [P, LT, TILE], F32R)
            acth = sb(s, "acth", [P, F0, TILE], F32R)
            actl = sb(s, "actl", [P, F0, TILE], F32R)
            raw = sb(s, "raw", [P, RAW, PANB * P])
            ph = sb(s, "ph", [P, 2, PANB * P], F32R)
            pl = sb(s, "pl", [P, 2, PANB * P], F32R)
            tmh = sb(s, "tmh", [P, 2, TILE], F32R)
            tml = sb(s, "tml", [P, 2, TILE], F32R)

        ps = ctx.enter_context(nc.psum_tensor("ps", [P, 8, 512], F32))

        par_in = sem("par_in")
        ids_in = sem("ids_in")
        consts = sem("consts")
        zero_set = sem("zero_set")
        zero_out = sem("zero_out")
        dve_link = sem("dve_link")
        half_arg = sem("half_arg")
        half_sin = sem("half_sin")
        u_in = [sem(f"u_in{i}") for i in range(2)]
        toep_in = [sem(f"toep_in{i}") for i in range(2)]
        mag_arg = sem("mag_arg")
        exp_done = sem("exp_done")
        sin_arg = sem("sin_arg")
        sin_done = sem("sin_done")
        ge_ready = sem("ge_ready")
        kmm_done = sem("kmm_done")
        k_copied = sem("k_copied")
        k_ready = sem("k_ready")
        k_out = sem("k_out")
        conv_done = sem("conv_done")
        conv_free = sem("conv_free")
        x1_done = sem("x1_done")
        w_in = [sem(f"w_in{i}") for i in range(WC)]
        table_ready = sem("table_ready")
        ident_set = sem("ident_set")
        mask_set = sem("mask_set")
        w_hi = sem("w_hi")
        w_lo = sem("w_lo")
        chunk_done = sem("chunk_done")
        rows_hi = sem("rows_hi")
        rows_cut = sem("rows_cut")
        prod_copied = sem("prod_copied")
        turned = sem("turned")
        step_added = sem("step_added")
        lora_out = sem("lora_out")
        raw_in = [sem(f"raw_in{i}") for i in range(RAW)]
        hi_ready = sem("hi_ready")
        lo_ready = sem("lo_ready")
        panel_done = sem("panel_done")
        rows_done = sem("rows_done")
        xh_ready = sem("xh_ready")
        xl_ready = sem("xl_ready")
        th_ready = sem("th_ready")
        t_ready = sem("t_ready")
        sig_ready = sem("sig_ready")
        silu_ready = sem("silu_ready")
        hid_ready = sem("hid_ready")
        act_ready = sem("act_ready")
        d_added = sem("d_added")
        y_out = sem("y_out")

        block = ctx.enter_context(nc.Block())
        PAIRS = H // 2
        CONVB = 4
        KBANK = 6

        def bank(i):
            return ps[:, i, :]

        @block.sync
        def _(sp):
            sp.dma_start(par[:], ins["params"]).then_inc(par_in, 16)
            sp.dma_start(drow[:], ins["D"]).then_inc(par_in, 16)
            sp.dma_start(leni[:], ins["length"].to_broadcast([P, B])).then_inc(par_in, 16)
            sp.dma_start(ids[:], ins["ids"]).then_inc(ids_in, 16)
            sp.dma_start(picki[:], ins["ids"][:, 0:2 * B].rearrange("o (l b) -> (o l) b", l=2)
                         ).then_inc(ids_in, 16)
            sp.wait_ge(zero_set, 1)
            sp.dma_start(kpad[:, 0:P], zrow[:]).then_inc(zero_out, 16)

            def load_inputs(g, i):
                sp.dma_start(u[:, i], ins["u"][:, bass.ds(g * UG, UG)]).then_inc(u_in[i], 16)
                sp.dma_start(urev[:, i], ins["urev"][:, bass.ds(g * UG, UG)]).then_inc(u_in[i], 16)

            def load_toeplitz(g, i):
                base = kpad[bass.ds(g * TG, TG), 1:1 + L]
                dims = [[1, P], [KPAD, TG], [1, L]]
                src = bass.AP(tensor=base.tensor, offset=base.offset, ap=dims)
                sp.dma_start(toep[:, i], src).then_inc(toep_in[i], 16)

            load_inputs(0, 0)
            load_inputs(1, 1)
            sp.wait_ge(zero_out, 16)
            for i in range(2):
                sp.wait_ge(k_out, 16)
                load_toeplitz(i, i)
            with sp.Fori(0, NCHUNK - 1) as c:
                for i in range(2):
                    sp.wait_ge(conv_done, c * (CH // 2) + (i + 1) * (TG // 2))
                    load_toeplitz(c * 4 + 2 + i, i)
                for i in range(2):
                    sp.wait_ge(x1_done, c * (CH // 2) + (i + 1) * (UG // 2))
                    load_inputs(c * 2 + 2 + i, i)
                    sp.wait_ge(conv_done, c * (CH // 2) + (i + 3) * (TG // 2))
                    if i == 0:
                        sp.wait_ge(k_out, c * 16 + 32)
                    load_toeplitz(c * 4 + 4 + i, i)
            for i in range(2):
                sp.wait_ge(conv_done, (NCHUNK - 1) * (CH // 2) + (i + 1) * (TG // 2))
                load_toeplitz(4 * NCHUNK - 2 + i, i)

            sp.wait_ge(table_ready, 1)
            before = 0
            for layer, w in enumerate((ins["w1"], ins["w2"])):
                count = sp.value_load(turns[layer:layer + 1, 0:1], min_val=B // 4, max_val=STEPS // 2)
                with sp.Fori(0, count) as it:
                    for half in range(2):
                        pick = sp.value_load(table[layer:layer + 1, 0, bass.ds(it * 2 + half, 1)],
                                             min_val=0, max_val=NPICK - 1)
                        for c in range(WC):
                            sp.wait_ge(w_lo, (it * 2 + (before + half)) * WC + (c + 1))
                            sp.dma_start(W[:, c], w[bass.ds(pick, 1), c].rearrange("a p i o -> (a p) i o")
                                         ).then_inc(w_in[c], 16)
                before = count * 2

            def load(n, count, src, at=0, incs=32):
                width = src.shape[-1]
                sp.dma_start(raw[:, n % RAW, at:at + width], src).then_inc(raw_in[n % RAW], incs)

            def room(count):
                sp.wait_ge(lo_ready, count + 1)

            def load_adapter(n, count, t, k):
                room(count)
                load(n, count, lora_a[bass.ds(t, 1), k].rearrange("t p b w -> (t p) (b w)"))

            def load_down_adapter(n, t, first, tiles):
                room(t * NPAN + n)
                sp.dma_start(raw[:, n % RAW, 0:TB * tiles * R].rearrange("p (b w) -> p b w", b=TB),
                             lora_ad[bass.ds(t, 1), :, :, first * R:(first + tiles) * R]
                             .rearrange("t p b w -> (t p) b w")).then_inc(raw_in[n % RAW], 32)

            def load_gate_up(n, t, j, pan):
                room(t * NPAN + j * 4 + n)
                load(n, 0, ins["wgu"][bass.ds(pan, 1)].rearrange("a p w -> (a p) w"), incs=16)
                load(n, 0, lora_b[bass.ds(t, 1), bass.ds(pan, 1)].rearrange("t a p w -> (t a p) w"),
                     at=LT * P, incs=16)

            sp.wait_ge(lora_out, NTILE * TB * 16 * 5)
            sp.wait_ge(rows_done, 1)
            load_adapter(0, 0, 0, 0)
            load_adapter(1, 1, 0, 1)
            with sp.Fori(0, NTILE) as t:
                for k in range(2):
                    load_gate_up(2 + k, t, 0, k)
                with sp.Fori(0, F0 // 2 - 1) as j:
                    for k in range(4):
                        load_gate_up(4 + k, t, j, j * 4 + (2 + k))
                for k in range(2):
                    load_gate_up(AD0 - 2 + k, t, 0, 2 * F0 - 2 + k)
                load_down_adapter(AD0, t, 0, F0)
                for o in range(LT):
                    room(t * NPAN + (AD0 + 1 + o))
                    load(AD0 + 1 + o, 0, ins["wd0"][o])
                for k in range(2):
                    load_gate_up(GU1 + k, t, 0, 2 * F0 + k)
                with sp.Fori(0, F1 // 2 - 1) as j:
                    for k in range(4):
                        load_gate_up(GU1 + 2 + k, t, j, j * 4 + (2 * F0 + 2 + k))
                for k in range(2):
                    load_gate_up(AD1 - 2 + k, t, 0, 2 * FT - 2 + k)
                load_down_adapter(AD1, t, F0, F1)
                for o in range(LT):
                    room(t * NPAN + (AD1 + 1 + o))
                    load(AD1 + 1 + o, 0, ins["wd1"][o], incs=16)
                    load(AD1 + 1 + o, 0, lora_bd[bass.ds(t, 1), o].rearrange("t p w -> (t p) w"),
                         at=F1 * P, incs=16)
                for k in range(2):
                    load_adapter(NPAN + k, t * NPAN + (NPAN + k), (t + 1) % NTILE, k)

        @block.gpsimd
        def _(pool):
            pool.memset(zrow[:], 0.0).then_inc(zero_set, 1)
            pool.iota(kk[:, 0:KB], pattern=[[1, KB]], base=0, channel_multiplier=0,
                      allow_small_or_imprecise_dtypes=True).then_inc(consts, 1)
            pool.iota(kk[:, KB:2 * KB], pattern=[[KB, KB]], base=0, channel_multiplier=0,
                      allow_small_or_imprecise_dtypes=True).then_inc(consts, 1)
            pool.iota(lpos[:], pattern=[[P, LT]], base=0, channel_multiplier=1,
                      allow_small_or_imprecise_dtypes=True).then_inc(consts, 1)
            for i, (upper, lower) in enumerate(((0.25, 0.0), (math.pi / 2, 0.0), (2.0, -2.0))):
                pool.wait_ge(consts, 3 + 2 * i)
                pool.memset(quarter[0:NS, i:i + 1], upper).then_inc(consts, 1)
                pool.wait_ge(consts, 4 + 2 * i)
                pool.memset(quarter[NS:P, i:i + 1], lower).then_inc(consts, 1)
            pool.wait_ge(consts, 9)
            pool.memset(tri[:], 1.0).then_inc(consts, 1)
            pool.iota(seqs[:], pattern=[[1, B]], base=0, channel_multiplier=0,
                      allow_small_or_imprecise_dtypes=True).then_inc(consts, 1)
            pool.iota(steps[:], pattern=[[1, ROOM]], base=0, channel_multiplier=0,
                      allow_small_or_imprecise_dtypes=True).then_inc(consts, 1)
            for k in range(2):
                pool.iota(spare[:, k].rearrange("l (t u) -> l t u", u=2), pattern=[[0, ROOM // 2], [2 - k, 2]],
                          base=B, channel_multiplier=0,
                          allow_small_or_imprecise_dtypes=True).then_inc(consts, 1)
            pool.memset(X[:, B:B + SPARE], 0.0).then_inc(consts, 1)
            pool.wait_ge(consts, 15)
            pool.affine_select(out=tri[:], in_=tri[:], compare_op=ALU.is_ge, fill=0.0, base=-1,
                               pattern=[[1, B], [-1, B]], channel_multiplier=0).then_inc(consts, 1)

            pool.wait_ge(ids_in, 32)
            with pool.Fori(0, NTILE) as t:
                for b in range(TB):
                    pick = pool.value_load(ids[0:1, bass.ds(t * TB + (2 * B + b), 1)], min_val=0, max_val=15)
                    one, tile = bass.ds(pick, 1), bass.ds(t, 1)
                    for k in range(2):
                        pool.dma_start(lora_a[tile, k, :, b].rearrange("t p w -> (t p) w"),
                                       ins["lora_a"][one, k].rearrange("a p w -> (a p) w")).then_inc(lora_out, 16)
                    pool.dma_start(lora_ad[tile, :, b].rearrange("t p w -> (t p) w"),
                                   ins["lora_ad"][one].rearrange("a p w -> (a p) w")).then_inc(lora_out, 16)
                    pool.dma_start(lora_b[tile, :, b * R:(b + 1) * R].rearrange("t a r w -> (t a) (r w)"),
                                   ins["lora_b"][one].rearrange("a n r w -> (a n) (r w)")).then_inc(lora_out, 16)
                    pool.dma_start(lora_bd[tile, :, b * R:(b + 1) * R].rearrange("t a r w -> (t a) (r w)"),
                                   ins["lora_bd"][one].rearrange("a n r w -> (a n) (r w)")).then_inc(lora_out, 16)

            pool.wait_ge(step_added, 2)
            pool.memset(ident[:], 0.0).then_inc(ident_set, 1)
            pool.wait_ge(ident_set, 1)
            pool.affine_select(out=ident[:], in_=ident[:], compare_op=ALU.not_equal, fill=1.0, base=0,
                               pattern=[[-1, P]], channel_multiplier=1).then_inc(ident_set, 1)

            pool.wait_ge(rows_done, 1)
            pool.memset(lora_mask, 0.5).then_inc(mask_set, 1)
            pool.wait_ge(mask_set, 1)
            pool.affine_select(out=lora_mask, in_=lora_mask, compare_op=ALU.is_ge, fill=0.0, base=0,
                               pattern=[[-R, TB], [0, H]], channel_multiplier=1).then_inc(mask_set, 1)
            pool.wait_ge(mask_set, 2)
            pool.affine_select(out=lora_mask, in_=lora_mask, compare_op=ALU.is_ge, fill=0.0, base=R - 1,
                               pattern=[[R, TB], [0, H]], channel_multiplier=-1).then_inc(mask_set, 1)

            with pool.Fori(0, NTILE) as t:
                pool.wait_ge(d_added, t * (2 * LT) + 2 * LT)
                pool.dma_start(out[bass.ds(t, 1)].rearrange("t p b l h -> (t p) b l h"),
                               X[:, bass.ds(t * TB, TB)]).then_inc(y_out, 16)
            pool.wait_ge(y_out, 16 * NTILE)

        @block.scalar
        def _(act):
            act.wait_ge(half_arg, 1)
            nc.scalar.activation(ex[:, 8:10], ex[:, 8:10], ACT.Sin).then_inc(half_sin, 1)

            def sines(c):
                act.wait_ge(mag_arg, c + 1)
                nc.scalar.activation(mag[:], mag[:], ACT.Exp).then_inc(exp_done, 1)
                act.wait_ge(sin_arg, c + 1)
                nc.scalar.activation(sin1[:], red[:], ACT.Sin).then_inc(sin_done, 1)
                nc.scalar.activation(sin2[:], red2[:], ACT.Sin).then_inc(sin_done, 1)

            def kernel_out(c):
                act.wait_ge(kmm_done, c + 1)
                if not isinstance(c, int) or c > 0:
                    act.wait_ge(k_out, c * 16)
                nc.scalar.activation(ksb[:], ps[0:KB, KBANK, :].rearrange("a (c b) -> a c b", c=CH),
                                     ACT.Copy).then_inc(k_copied, 1)
                act.wait_ge(k_ready, c + 1)
                dst = kpad[bass.ds(c * CH, CH), P:KPAD].rearrange("c (a b) -> a c b", a=KB)
                act.dma_start(dst, ksb[:]).then_inc(k_out, 16)

            sines(0)
            kernel_out(0)
            with act.Fori(1, NCHUNK) as c:
                sines(c)
                kernel_out(c)

            def cut_chunk(g, c):
                act.wait_ge(w_in[c], (g + 1) * 16)
                act.wait_ge(chunk_done, g * WC + (c + 1))
                nc.scalar.activation(wh[:, c], W[:, c], ACT.Copy).then_inc(w_hi, 1)

            def copy_product(g, half, o):
                act.wait_ge(chunk_done, g * WC + (2 * o + 2 + WC))
                nc.scalar.activation(prod[:, half, o * WN:(o + 1) * WN], bank(2 * half + o),
                                     ACT.Copy).then_inc(prod_copied, 1)

            def step_rows_hi(s, half, added):
                seqs = [act.value_load(table[layer:layer + 1, 1 + k, bass.ds(s, 1)],
                                       min_val=0, max_val=B + SPARE - 1) for k in range(2)]
                act.wait_ge(step_added, added)
                for k, seq in enumerate(seqs):
                    nc.scalar.activation(rh[:, half, :, k * H:(k + 1) * H],
                                         X[:, bass.ds(seq, 1)].rearrange("p a l h -> p (a l) h"),
                                         ACT.Copy).then_inc(rows_hi, 1)

            def picked_turn(it, base, first):
                for half in range(2):
                    s = it * 2 + half
                    g = base + s
                    lag = not (first and half == 0)
                    cut_chunk(g, 0)
                    if lag:
                        copy_product(g - 1, 1 - half, 0)
                    cut_chunk(g, 1)
                    cut_chunk(g, 2)
                    if lag:
                        copy_product(g - 1, 1 - half, 1)
                    cut_chunk(g, 3)
                    step_rows_hi(s + 1, 1 - half, g + 2)

            act.wait_ge(table_ready, 1)
            base = 0
            for layer in range(2):
                count = act.value_load(turns[layer:layer + 1, 0:1], min_val=B // 4, max_val=STEPS // 2)
                step_rows_hi(0, 0, base + 2)
                picked_turn(0, base, True)
                with act.Fori(1, count) as it:
                    picked_turn(it, base, False)
                base = base + count * 2
                copy_product(base - 1, 1, 0)
                copy_product(base - 1, 1, 1)

            def come(n, t, j=0):
                act.wait_ge(raw_in[n % RAW], (t * (NPAN // RAW) + j + (n // RAW + 1)) * 32)
                act.wait_ge(panel_done, t * NPAN + j * 4 + (n + 1))

            def cut(n, blocks, t, j=0):
                come(n, t, j)
                nc.scalar.activation(ph[:, n % 2, 0:blocks * P], raw[:, n % RAW, 0:blocks * P],
                                     ACT.Copy).then_inc(hi_ready, 1)

            def cut_adapter(n, blocks, t):
                come(n, t)
                nc.scalar.activation(
                    ph[:, n % 2, 0:blocks * P].rearrange("p (k b r) -> p b k r", b=TB, r=R),
                    raw[:, n % RAW, 0:blocks * P].rearrange("p (b k r) -> p b k r", b=TB, r=R),
                    ACT.Copy).then_inc(hi_ready, 1)

            def cut_rows(t):
                nc.scalar.activation(xh[:].rearrange("p l (b h) -> p b l h", h=H),
                                     X[:, bass.ds(t * TB, TB)], ACT.Copy).then_inc(xh_ready, 1)

            def sigmoid(pair, n, t, j=0):
                act.wait_ge(panel_done, t * NPAN + j * 4 + (n + 3))
                nc.scalar.activation(hid[pair % 2], bank(GATE[pair % 2]),
                                     ACT.Sigmoid).then_inc(sig_ready, 1)

            act.wait_ge(rows_done, 1)
            cut_adapter(0, LT, 0)
            cut_adapter(1, LT, 0)
            cut_rows(0)
            with act.Fori(0, NTILE) as t:
                cut(2, LT + 1, t)
                cut(3, LT + 1, t)
                with act.Fori(0, F0 // 2 - 1) as j:
                    for k in range(2):
                        cut(4 + 2 * k, LT + 1, t, j)
                        cut(5 + 2 * k, LT + 1, t, j)
                        sigmoid(k, 3 + 2 * k, t, j)
                cut(AD0 - 2, LT + 1, t)
                cut(AD0 - 1, LT + 1, t)
                sigmoid(F0 - 2, AD0 - 3, t)
                cut_adapter(AD0, F0, t)
                cut(AD0 + 1, F0, t)
                sigmoid(F0 - 1, AD0 - 1, t)
                for o in range(1, LT):
                    cut(AD0 + 1 + o, F0, t)
                cut(GU1, LT + 1, t)
                cut(GU1 + 1, LT + 1, t)
                with act.Fori(0, F1 // 2 - 1) as j:
                    for k in range(2):
                        cut(GU1 + 2 + 2 * k, LT + 1, t, j)
                        cut(GU1 + 3 + 2 * k, LT + 1, t, j)
                        sigmoid(F0 + k, GU1 + 1 + 2 * k, t, j)
                cut(AD1 - 2, LT + 1, t)
                cut(AD1 - 1, LT + 1, t)
                sigmoid(FT - 2, AD1 - 3, t)
                cut_adapter(AD1, F1, t)
                cut(AD1 + 1, F1 + 1, t)
                sigmoid(FT - 1, AD1 - 1, t)
                cut(AD1 + 2, F1 + 1, t)
                cut_rows((t + 1) % NTILE)
                for o in range(2, LT):
                    cut(AD1 + 1 + o, F1 + 1, t)
                for k in range(2):
                    cut_adapter(NPAN + k, LT, t)

        @block.vector
        def _(dve):
            V = nc.vector
            linked = [0]

            def link(ins, before=0):
                linked[0] += 1
                ins.then_inc(dve_link, 1)
                dve.wait_ge(dve_link, before + linked[0])

            def round_turns(t, before=0):
                link(V.tensor_scalar_add(t, t, MAGIC), before)
                link(V.tensor_scalar_add(t, t, -MAGIC), before)

            def expm1_of(x, n, r, q, two):
                link(V.tensor_scalar(n, x, 1 / math.log(2), None, ALU.mult))
                round_turns(n)
                link(V.tensor_scalar(n, n, -126.0, 127.0, ALU.max, ALU.min))
                link(V.scalar_tensor_tensor(out=r, in0=n, scalar=-LN2_1, in1=x, op0=ALU.mult, op1=ALU.add))
                link(V.scalar_tensor_tensor(out=r, in0=n, scalar=-LN2_2, in1=r, op0=ALU.mult, op1=ALU.add))
                link(V.tensor_scalar(q, r, 1 / 40320, None, ALU.mult))
                for d in (5040, 720, 120, 24, 6, 2, 1):
                    link(V.scalar_tensor_tensor(out=q, in0=q, scalar=1 / d, in1=r, op0=ALU.add, op1=ALU.mult))
                link(V.tensor_scalar(two, n, 127.0, float(2 ** 23), ALU.add, ALU.mult))

            def tt(out_, a, b, op, before=0):
                link(V.tensor_tensor(out=out_, in0=a, in1=b, op=op), before)

            V.memset(tick[:, 0:1], 0.0).then_inc(conv_free, CONVB)
            link(V.memset(ex[:], 0.0))
            dve.wait_ge(par_in, 48)
            dve.wait_ge(consts, 9)

            two = exi[:, 0:2].bitcast(F32)
            expm1_of(par[:, 0:2], ex[:, 0:2], ex[:, 2:4], ex[:, 4:6], exi[:, 0:2])
            tt(ex[:, 6:8], ex[:, 4:6], two, ALU.mult)
            tt(ex[:, 6:8], ex[:, 6:8], two, ALU.add)
            link(V.tensor_scalar(ex[:, 6], ex[:, 6], -1.0, None, ALU.mult))
            ar, dt, ai = ex[:, 6], ex[:, 7], par[:, 2]
            tt(dta[:, 0], ar, dt, ALU.mult)
            tt(dta[:, 1], ai, dt, ALU.mult)
            expm1_of(dta[:, 0], ex[:, 0], ex[:, 1], ex[:, 2], exi[:, 0])
            one = exi[:, 0].bitcast(F32)
            tt(ex[:, 2], ex[:, 2], one, ALU.mult)
            link(V.scalar_tensor_tensor(out=ex[:, 3], in0=one, scalar=-1.0, in1=ex[:, 2],
                                        op0=ALU.add, op1=ALU.add))
            link(V.tensor_scalar(ex[:, 10], dta[:, 1], 0.5, None, ALU.mult))
            link(V.tensor_scalar(ex[:, 11], dta[:, 1], 0.5, None, ALU.mult))
            link(V.tensor_scalar(ex[:, 4:6], ex[:, 10:12], 1 / TWO_PI, None, ALU.mult))
            link(V.tensor_scalar_add(ex[:, 5], ex[:, 5], 0.25))
            round_turns(ex[:, 4:6])
            for i, part in enumerate((TWO_PI_1, TWO_PI_2, TWO_PI_3)):
                link(V.scalar_tensor_tensor(out=ex[:, 8:10], in0=ex[:, 4:6], scalar=-part,
                                            in1=ex[:, 10:12] if i == 0 else ex[:, 8:10],
                                            op0=ALU.mult, op1=ALU.add))
            link(V.tensor_scalar_add(ex[:, 9], ex[:, 9], math.pi / 2))
            V.tensor_scalar(ex[:, 8:10], ex[:, 8:10], PI, -PI, ALU.min, ALU.max).then_inc(half_arg, 1)
            dve.wait_ge(half_sin, 1)
            em, s2, c2, cr, ci = ex[:, 3], ex[:, 8], ex[:, 9], par[:, 3], par[:, 4]
            link(V.tensor_scalar_add(ex[:, 0], em, 1.0))
            link(V.scalar_tensor_tensor(out=ex[:, 0], in0=ex[:, 0], scalar=-2.0, in1=s2,
                                        op0=ALU.mult, op1=ALU.mult))
            tt(ex[:, 1], ex[:, 0], s2, ALU.mult)
            tt(ex[:, 1], ex[:, 1], em, ALU.add)
            tt(ex[:, 2], ex[:, 0], c2, ALU.mult)
            tt(ex[:, 4], cr, ex[:, 1], ALU.mult)
            tt(ex[:, 5], ci, ex[:, 2], ALU.mult)
            tt(ex[:, 4], ex[:, 4], ex[:, 5], ALU.add)
            tt(ex[:, 5], ci, ex[:, 1], ALU.mult)
            tt(ex[:, 8], cr, ex[:, 2], ALU.mult)
            tt(ex[:, 5], ex[:, 5], ex[:, 8], ALU.subtract)
            tt(ex[:, 8], ar, ar, ALU.mult)
            tt(ex[:, 9], ai, ai, ALU.mult)
            tt(ex[:, 8], ex[:, 8], ex[:, 9], ALU.add)
            link(V.reciprocal(ex[:, 8], ex[:, 8]))
            link(V.tensor_scalar(ex[:, 8], ex[:, 8], quarter[:, 2:3], None, ALU.mult))
            for o, a, b, op in ((0, ex[:, 4], ex[:, 5], ALU.add), (1, ex[:, 5], ex[:, 4], ALU.subtract)):
                tt(ex[:, 9], a, ar, ALU.mult)
                tt(ex[:, 10], b, ai, ALU.mult)
                tt(ex[:, 9], ex[:, 9], ex[:, 10], op)
                tt(ct[:, o], ex[:, 9], ex[:, 8], ALU.mult)
            link(V.tensor_copy(lenf[:], leni[:]))
            tt(lmask[:], lenf[:].unsqueeze(1).to_broadcast([P, LT, B]),
               lpos[:].unsqueeze(2).to_broadcast([P, LT, B]), ALU.is_gt)

            def over_k(a, c, n):
                return a[:, bass.ds(c * CH, CH)].unsqueeze(2).to_broadcast([P, CH, n])

            all_k = kk[:].unsqueeze(1).to_broadcast([P, CH, 2 * KB])

            def phases(c, before=0):
                V.tensor_tensor(out=mag[:], in0=over_k(dta[:, 0], c, 2 * KB), in1=all_k,
                                op=ALU.mult).then_inc(mag_arg, 1)
                tt(ang[:], over_k(dta[:, 1], c, 2 * KB), all_k, ALU.mult, before)
                link(V.tensor_scalar(turn[:], ang[:], 1 / TWO_PI, quarter[:, 0:1], ALU.mult, ALU.add), before)
                round_turns(turn[:], before)
                for i, part in enumerate((TWO_PI_1, TWO_PI_2, TWO_PI_3)):
                    link(V.scalar_tensor_tensor(out=red[:], in0=turn[:], scalar=-part,
                                                in1=ang[:] if i == 0 else red[:],
                                                op0=ALU.mult, op1=ALU.add), before)

            def quarter_turns(c, before=0):
                link(V.tensor_scalar(red[:], red[:], quarter[:, 1:2], PI, ALU.add, ALU.min), before)
                link(V.tensor_scalar(red[:], red[:], -PI, None, ALU.max), before)
                r = red[:, :, KB:2 * KB]
                link(V.tensor_scalar(turn[:, :, 0:KB], r, PI / 2, -TWO_PI, ALU.is_gt, ALU.mult), before)
                link(V.scalar_tensor_tensor(out=red2[:], in0=r, scalar=PI / 2, in1=turn[:, :, 0:KB],
                                            op0=ALU.add, op1=ALU.add), before)
                V.tensor_scalar(red2[:], red2[:], PI, -PI, ALU.min, ALU.max).then_inc(sin_arg, 1)

            def powers(c, before=0):
                dve.wait_ge(exp_done, c + 1)
                dve.wait_ge(sin_done, c * 2 + 2)
                if not isinstance(c, int):
                    dve.wait_ge(kmm_done, c)
                V.tensor_tensor(out=ge[:, :, 0:KB], in0=sin1[:, :, 0:KB], in1=mag[:, :, 0:KB], op=ALU.mult)
                V.tensor_tensor(out=sin1[:, :, KB:2 * KB], in0=sin1[:, :, KB:2 * KB],
                                in1=mag[:, :, KB:2 * KB], op=ALU.mult)
                tt(sin2[:], sin2[:], mag[:, :, KB:2 * KB], ALU.mult, before)
                V.tensor_tensor(out=sin1[:, :, KB:2 * KB], in0=sin1[:, :, KB:2 * KB],
                                in1=over_k(ct[:, 0], c, KB), op=ALU.mult)
                tt(sin2[:], sin2[:], over_k(ct[:, 1], c, KB), ALU.mult, before)
                V.tensor_tensor(out=ge[:, :, KB:2 * KB], in0=sin1[:, :, KB:2 * KB], in1=sin2[:],
                                op=ALU.add).then_inc(ge_ready, 1)

            def add_d(c):
                dve.wait_ge(k_copied, c + 1)
                V.tensor_tensor(out=ksb[0:1, :, 0:1], in0=ksb[0:1, :, 0:1],
                                in1=drow[0:1, bass.ds(c * CH, CH)].unsqueeze(2), op=ALU.add).then_inc(k_ready, 1)

            def add_conv(c, i):
                q = c * (CH // 2) + i
                dve.wait_ge(conv_done, q + 1)
                mi = masked[:, i % 2].rearrange("p e l b -> p e (l b)")
                V.tensor_tensor(out=mi, in0=bank(i % CONVB).rearrange("p (e w) -> p e w", e=2),
                                in1=lmask[:].rearrange("p l b -> p (l b)").unsqueeze(1)
                                .to_broadcast([P, 2, LT * B]), op=ALU.mult).then_inc(conv_free, 1)
                dve.wait_ge(conv_free, q + (CONVB + 1))
                chan = 2 * (i % (UG // 2))
                V.tensor_tensor(out=X[:, 0:B].rearrange("p b l h -> p h l b")[:, bass.ds(c * CH + 2 * i, 2)],
                                in0=masked[:, i % 2], in1=u[:, i // (UG // 2), chan:chan + 2],
                                op=ALU.add).then_inc(x1_done, 1)

            phases(0)
            quarter_turns(0)
            powers(0)
            add_d(0)

            dve.wait_ge(ids_in, 32)
            dve.wait_ge(consts, 16)
            over_b = lambda a, n: a.unsqueeze(1).to_broadcast([2, n, B])
            of_b = lambda a: a.unsqueeze(2).to_broadcast([2, B, B])
            pick, rank, floor, odd, even, step = (pk[:, i] for i in range(6))
            link(V.tensor_copy(pick, picki[:]))
            tt(pair[:], of_b(pick), over_b(pick, B), ALU.is_equal)
            tt(pair[:], pair[:], tri[:], ALU.mult)
            link(V.reduce_sum(rank, pair[:], axis=mybir.AxisListType.X))
            link(V.tensor_scalar(floor, rank, 0.5, -0.25, ALU.mult, ALU.add))
            round_turns(floor)
            link(V.scalar_tensor_tensor(out=odd, in0=floor, scalar=-2.0, in1=rank, op0=ALU.mult, op1=ALU.add))
            link(V.tensor_scalar(even, odd, -1.0, 1.0, ALU.mult, ALU.add))
            tt(pair[:], of_b(pick), over_b(pick, B), ALU.is_gt)
            tt(pair[:], pair[:], over_b(even, B), ALU.mult)
            link(V.reduce_sum(step, pair[:], axis=mybir.AxisListType.X))
            tt(step, step, floor, ALU.add)
            link(V.reduce_max(found[:, 0, 0:1], step, axis=mybir.AxisListType.X))
            link(V.tensor_scalar(found[:, 0, 0:1], found[:, 0, 0:1], 0.5, 0.75, ALU.mult, ALU.add))
            round_turns(found[:, 0, 0:1])
            link(V.tensor_copy(turns[:], found[:, 0, 0:1]))
            tt(hit[:, 1], over_b(step, ROOM), steps[:].unsqueeze(2).to_broadcast([2, ROOM, B]), ALU.is_equal)
            tt(hit[:, 0], hit[:, 1], over_b(even, ROOM), ALU.mult)
            tt(hit[:, 1], hit[:, 1], over_b(odd, ROOM), ALU.mult)
            link(V.reduce_sum(found[:, 0:2], hit[:], axis=mybir.AxisListType.X))
            tt(pair[:, 0:ROOM], hit[:, 0], over_b(pick, ROOM), ALU.mult)
            link(V.reduce_sum(found[:, 2], pair[:, 0:ROOM], axis=mybir.AxisListType.X))
            for k in range(2):
                tt(hit[:, k], hit[:, k], over_b(seqs[:], ROOM), ALU.mult)
            link(V.reduce_sum(found[:, 3:5], hit[:], axis=mybir.AxisListType.X))
            link(V.tensor_scalar(found[:, 0:2], found[:, 0:2], -1.0, 1.0, ALU.mult, ALU.add))
            tt(found[:, 0:2], found[:, 0:2], spare[:], ALU.mult)
            tt(found[:, 3:5], found[:, 3:5], found[:, 0:2], ALU.add)
            V.tensor_copy(table[:], found[:, 2:5]).then_inc(table_ready, 1)

            setup_links = linked[0]
            with dve.Fori(0, NCHUNK - 1) as c:
                linked[0] = setup_links
                before = c * CHUNK_LINKS
                add_conv(c, 0)
                phases(c + 1, before)
                add_conv(c, 1)
                add_conv(c, 2)
                quarter_turns(c + 1, before)
                add_conv(c, 3)
                powers(c + 1, before)
                add_conv(c, 4)
                add_conv(c, 5)
                add_d(c + 1)
                add_conv(c, 6)
                add_conv(c, 7)
                assert linked[0] - setup_links == CHUNK_LINKS
            for i in range(CH // 2):
                add_conv(NCHUNK - 1, i)

            dve.wait_ge(x1_done, PAIRS)
            V.memset(tick[:, 1:2], 0.0).then_inc(w_lo, WC)
            V.memset(tick[:, 2:3], 0.0).then_inc(chunk_done, WC)
            V.memset(tick[:, 3:4], 0.0).then_inc(step_added, 2)

            def cut_chunk(g, c):
                dve.wait_ge(w_hi, g * WC + (c + 1))
                V.tensor_tensor(out=wl[:, c], in0=W[:, c], in1=wh[:, c].bitcast(F32),
                                op=ALU.subtract).then_inc(w_lo, 1)

            def place(s, k):
                return dve.value_load(table[layer:layer + 1, 1 + k, bass.ds(s, 1)],
                                      min_val=0, max_val=B + SPARE - 1)

            def step_rows_lo(s, g, half):
                for k in range(2):
                    seq = place(s, k)
                    dve.wait_ge(rows_hi, (g + layer) * 2 + (k + 1))
                    mine = slice(k * H, (k + 1) * H)
                    V.tensor_tensor(out=rl[:, half, :, mine],
                                    in0=X[:, bass.ds(seq, 1)].rearrange("p a l h -> p (a l) h"),
                                    in1=rh[:, half, :, mine].bitcast(F32), op=ALU.subtract).then_inc(rows_cut, 1)

            def add_step(s, g):
                for k in range(2):
                    seq = place(s, k)
                    dve.wait_ge(turned, g + 1)
                    rows = X[:, bass.ds(seq, 1)].rearrange("p a l h -> p (a l) h")
                    ins_ = V.tensor_tensor(out=rows, in0=ps[:, TURN:TURN + 2].rearrange(
                        "p c (l w) -> p (c l) w", w=2 * H)[:, :, k * H:(k + 1) * H], in1=rows, op=ALU.add)
                ins_.then_inc(step_added, 1)

            dve.wait_ge(table_ready, 1)
            base = 0
            for layer in range(2):
                count = dve.value_load(turns[layer:layer + 1, 0:1], min_val=B // 4, max_val=STEPS // 2)
                step_rows_lo(0, base, 0)
                for half in range(2):
                    for c in range(WC):
                        cut_chunk(base + half, c)
                    if half == 1:
                        add_step(0, base)
                    step_rows_lo(half + 1, base + (half + 1), 1 - half)
                with dve.Fori(1, count) as it:
                    for half in range(2):
                        s = it * 2 + half
                        for c in range(WC):
                            cut_chunk(base + s, c)
                        add_step(s - 1, base + s - 1)
                        step_rows_lo(s + 1, base + s + 1, 1 - half)
                base = base + count * 2
                add_step(count * 2 - 1, base - 1)
            dve.wait_ge(step_added, base + 2)
            V.memset(tick[:, 4:5], 0.0).then_inc(panel_done, 2)
            V.memset(tick[:, 5:6], 0.0).then_inc(lo_ready, RAW)
            V.memset(tick[:, 6:7], 0.0).then_inc(rows_done, 1)

            def cut(n, blocks, t, j=0):
                dve.wait_ge(hi_ready, t * NPAN + j * 4 + (n + 1))
                V.tensor_tensor(out=pl[:, n % 2, 0:blocks * P], in0=raw[:, n % RAW, 0:blocks * P],
                                in1=ph[:, n % 2, 0:blocks * P].bitcast(F32),
                                op=ALU.subtract).then_inc(lo_ready, 1)

            def cut_adapter(n, blocks, t):
                dve.wait_ge(hi_ready, t * NPAN + (n + 1))
                way = dict(b=TB, r=R)
                V.tensor_tensor(
                    out=pl[:, n % 2, 0:blocks * P].rearrange("p (k b r) -> p b k r", **way),
                    in0=raw[:, n % RAW, 0:blocks * P].rearrange("p (b k r) -> p b k r", **way),
                    in1=ph[:, n % 2, 0:blocks * P].bitcast(F32).rearrange("p (k b r) -> p b k r", **way),
                    op=ALU.subtract).then_inc(lo_ready, 1)

            def cut_rows(t, count):
                dve.wait_ge(xh_ready, count)
                way = dict(h=H)
                V.tensor_tensor(out=xl[:].rearrange("p l (b h) -> p b l h", **way), in0=X[:, bass.ds(t * TB, TB)],
                                in1=xh[:].bitcast(F32).rearrange("p l (b h) -> p b l h", **way),
                                op=ALU.subtract).then_inc(xl_ready, 1)

            def adapter(k, count, n, bk, t):
                dve.wait_ge(panel_done, t * NPAN + (n + 3))
                mask, prod, part = lora_mask.rearrange("p b h -> p (b h)"), bank(bk), hid[count % 2]
                V.tensor_tensor(out=part, in0=prod, in1=mask, op=ALU.mult)
                V.tensor_tensor(out=tmh[:, k], in0=prod, in1=mask, op=ALU.mult).then_inc(th_ready, 1)
                dve.wait_ge(th_ready, t * 3 + (count + 1))
                V.tensor_tensor(out=tml[:, k], in0=part, in1=tmh[:, k].bitcast(F32),
                                op=ALU.subtract).then_inc(t_ready, 1)

            def hidden(pair, at, n, t, j=0):
                count, two_ = t * FT + j * 2 + (pair + 1), pair % 2
                dve.wait_ge(panel_done, t * NPAN + j * 4 + (n + 3))
                dve.wait_ge(sig_ready, count)
                V.tensor_tensor(out=hid[two_], in0=hid[two_], in1=bank(GATE[two_]),
                                op=ALU.mult).then_inc(silu_ready, 1)
                dve.wait_ge(silu_ready, count)
                one = bass.ds(j * 2 + at, 1) if not isinstance(j, int) else slice(at, at + 1)
                hi, lo = acth[:, one].rearrange("p a w -> p (a w)"), actl[:, one].rearrange("p a w -> p (a w)")
                V.tensor_tensor(out=hi, in0=hid[two_], in1=bank(GATE[two_] + 1), op=ALU.mult)
                V.tensor_tensor(out=hid[two_], in0=hid[two_], in1=bank(GATE[two_] + 1),
                                op=ALU.mult).then_inc(hid_ready, 1)
                dve.wait_ge(hid_ready, count)
                V.tensor_tensor(out=lo, in0=hid[two_], in1=hi.bitcast(F32),
                                op=ALU.subtract).then_inc(act_ready, 1)

            def down(o, n, t):
                dve.wait_ge(panel_done, t * NPAN + (n + 3))
                rows = X[:, bass.ds(t * TB, TB), o]
                V.tensor_tensor(out=rows, in0=bank(DOWN[o % 3]).rearrange("p (b h) -> p b h", h=H), in1=rows, op=ALU.add).then_inc(d_added, 1)

            dve.wait_ge(mask_set, 3)
            cut_adapter(0, LT, 0)
            cut_adapter(1, LT, 0)
            cut_rows(0, 1)
            with dve.Fori(0, NTILE) as t:
                cut(2, LT + 1, t)
                adapter(0, 0, 0, BANK_A, t)
                cut(3, LT + 1, t)
                adapter(1, 1, 1, BANK_AD, t)
                with dve.Fori(0, F0 // 2 - 1) as j:
                    for k in range(2):
                        cut(4 + 2 * k, LT + 1, t, j)
                        cut(5 + 2 * k, LT + 1, t, j)
                        hidden(k, k, 3 + 2 * k, t, j)
                cut(AD0 - 2, LT + 1, t)
                cut(AD0 - 1, LT + 1, t)
                hidden(F0 - 2, F0 - 2, AD0 - 3, t)
                cut_adapter(AD0, F0, t)
                cut(AD0 + 1, F0, t)
                hidden(F0 - 1, F0 - 1, AD0 - 1, t)
                cut(AD0 + 2, F0, t)
                for o in range(2, LT):
                    cut(AD0 + 1 + o, F0, t)
                    down(o - 2, AD0 - 1 + o, t)
                cut(GU1, LT + 1, t)
                down(LT - 2, GU1 - 2, t)
                cut(GU1 + 1, LT + 1, t)
                down(LT - 1, GU1 - 1, t)
                with dve.Fori(0, F1 // 2 - 1) as j:
                    for k in range(2):
                        cut(GU1 + 2 + 2 * k, LT + 1, t, j)
                        cut(GU1 + 3 + 2 * k, LT + 1, t, j)
                        hidden(F0 + k, k, GU1 + 1 + 2 * k, t, j)
                cut(AD1 - 2, LT + 1, t)
                cut(AD1 - 1, LT + 1, t)
                hidden(FT - 2, F1 - 2, AD1 - 3, t)
                cut_adapter(AD1, F1, t)
                cut(AD1 + 1, F1 + 1, t)
                hidden(FT - 1, F1 - 1, AD1 - 1, t)
                cut(AD1 + 2, F1 + 1, t)
                adapter(0, 2, AD1, BANK_AD, t)
                cut_rows((t + 1) % NTILE, t + 2)
                for o in range(2, LT):
                    cut(AD1 + 1 + o, F1 + 1, t)
                    down(o - 2, AD1 - 1 + o, t)
                for k in range(2):
                    cut_adapter(NPAN + k, LT, t)
                    down(LT - 2 + k, NPAN - 2 + k, t)

        @block.tensor
        def _(pe):
            mm = nc.tensor.matmul

            def kernels(c):
                pe.wait_ge(ge_ready, c + 1)
                if not isinstance(c, int):
                    pe.wait_ge(k_copied, c)
                for h in range(CH):
                    last = mm(ps[0:KB, KBANK, h * KB:(h + 1) * KB], lhsT=ge[:, h, KB:2 * KB],
                              rhs=ge[:, h, 0:KB], start=True, stop=True)
                last.then_inc(kmm_done, 1)

            def convolve(c, g):
                half = g // 2
                pe.wait_ge(toep_in[g % 2], (c * 2 + (half + 1)) * 16)
                pe.wait_ge(u_in[half], (c + 1) * 32)
                for i in range(2):
                    pair = 2 * g + i
                    pe.wait_ge(conv_free, c * (CH // 2) + (pair + 1))
                    for e in range(2):
                        tile = toep[:, g % 2, 2 * i + e]
                        rows = urev[:, half, (pair % 4) * 2 + e].rearrange("p l b -> p (l b)")
                        for d in range(LT):
                            n = (LT - d) * B
                            last = mm(ps[:, pair % CONVB, (e + 1) * LT * B - n:(e + 1) * LT * B],
                                      lhsT=tile[:, d * P:(d + 1) * P], rhs=rows[:, 0:n],
                                      start=d == 0, stop=d == LT - 1)
                    last.then_inc(conv_done, 1)

            kernels(0)
            with pe.Fori(0, NCHUNK - 1) as c:
                convolve(c, 0)
                convolve(c, 1)
                convolve(c, 2)
                kernels(c + 1)
                convolve(c, 3)
            for g in range(4):
                convolve(NCHUNK - 1, g)

            def chunk(g, half, c):
                pe.wait_ge(w_lo, g * WC + (c + 1 + WC))
                to = bank(2 * half + c // 2)
                for k in range(WK):
                    at = (c % 2) * WK + k
                    first, end = at == 0, at == LT - 1
                    mm(to, lhsT=rh[:, half, at], rhs=wh[:, c, k], start=first, stop=False)
                    mm(to, lhsT=rh[:, half, at], rhs=wl[:, c, k], start=False, stop=False)
                    last = mm(to, lhsT=rl[:, half, at], rhs=wh[:, c, k], start=False, stop=end)
                last.then_inc(chunk_done, 1)

            def turn_product(g, half):
                pe.wait_ge(prod_copied, g * 2 + 2)
                pe.wait_ge(step_added, g + 2)
                for o in range(LT):
                    last = nc.tensor.transpose(ps[:, TURN + o // 4, (o % 4) * P:(o % 4 + 1) * P],
                                               prod[:, half, o * P:(o + 1) * P], ident[:])
                last.then_inc(turned, 1)

            def picked_turn(it, base, first):
                for half in range(2):
                    g = base + it * 2 + half
                    pe.wait_ge(rows_cut, (g + layer) * 2 + 2)
                    chunk(g, half, 0)
                    chunk(g, half, 1)
                    if not (first and half == 0):
                        turn_product(g - 1, 1 - half)
                    chunk(g, half, 2)
                    chunk(g, half, 3)

            pe.wait_ge(ident_set, 2)
            pe.wait_ge(table_ready, 1)
            base = 0
            for layer in range(2):
                count = pe.value_load(turns[layer:layer + 1, 0:1], min_val=B // 4, max_val=STEPS // 2)
                picked_turn(0, base, True)
                with pe.Fori(1, count) as it:
                    picked_turn(it, base, False)
                base = base + count * 2
                turn_product(base - 1, 1)

            def panel(n, bk, blocks, hi, lo, t, j=0, start=True, stop=True, extra=None, ready=None):
                pe.wait_ge(lo_ready, t * NPAN + j * 4 + (n + RAW + 1))
                moving = [(hi[:, k], lo[:, k]) for k in range(blocks)] + ([extra[0]] if extra else [])
                for k, (mh, ml) in enumerate(moving):
                    if extra and k == blocks:
                        pe.wait_ge(*extra[1])
                    if ready and k in ready:
                        pe.wait_ge(act_ready, ready[k])
                    wh, wl = ph[:, n % 2, k * P:(k + 1) * P], pl[:, n % 2, k * P:(k + 1) * P]
                    first, end = start and k == 0, stop and k == len(moving) - 1
                    mm(bank(bk), lhsT=wh, rhs=mh, start=first, stop=False)
                    mm(bank(bk), lhsT=wh, rhs=ml, start=False, stop=False)
                    last = mm(bank(bk), lhsT=wl, rhs=mh, start=False, stop=end)
                last.then_inc(panel_done, 1)

            def gate_up(pair, n, t, j=0):
                for k in range(2):
                    panel(n + k, GATE[pair % 2] + k, LT, xh, xl, t, j,
                          extra=((tmh[:, k], tml[:, k]), (t_ready, t * 3 + (k + 1))))

            with pe.Fori(0, NTILE) as t:
                pe.wait_ge(xl_ready, t + 1)
                panel(0, BANK_A, LT, xh, xl, t)
                panel(1, BANK_AD, LT, xh, xl, t)
                with pe.Fori(0, F0 // 2) as j:
                    for k in range(2):
                        gate_up(k, 2 + 2 * k, t, j)
                done = lambda k: t * FT + (k + 1)
                panel(AD0, BANK_AD, F0, acth, actl, t, stop=False,
                      ready={0: done(F0 - 3), F0 - 2: done(F0 - 2), F0 - 1: done(F0 - 1)})
                for o in range(LT):
                    panel(AD0 + 1 + o, DOWN[o % 3], F0, acth, actl, t)
                with pe.Fori(0, F1 // 2) as j:
                    for k in range(2):
                        gate_up(k, GU1 + 2 * k, t, j)
                panel(AD1, BANK_AD, F1, acth, actl, t, start=False,
                      ready={0: done(FT - 3), F1 - 2: done(FT - 2), F1 - 1: done(FT - 1)})
                for o in range(LT):
                    panel(AD1 + 1 + o, DOWN[o % 3], F1, acth, actl, t,
                          extra=((tmh[:, 0], tml[:, 0]), (t_ready, t * 3 + 3)))


def kernel(**inputs):
    import numpy as np
    import concourse.bacc as bacc
    from concourse.bass_utils import run_bass_kernel_spmd

    f = {k.replace("_cond", ""): np.asarray(v) for k, v in inputs.items()}

    x = f["x"].reshape(B, H, LT, P)
    u = x.transpose(3, 1, 2, 0)
    state = [f["L0_log_A_real"].T, np.broadcast_to(f["L0_log_dt"][None, :], (NS, H)), f["L0_A_imag"].T,
             f["L0_C"][:, :, 0].T, f["L0_C"][:, :, 1].T]
    params = np.stack(state, axis=1)
    picked = lambda w: w.reshape(NPICK, 2, WN, 2, WK, P).transpose(0, 1, 3, 5, 4, 2).reshape(
        NPICK, WC, P, WK, WN)
    pad = FT * P - FF
    tiles = lambda w: np.pad(w, ((0, pad), (0, 0))).reshape(FT, P, LT, P).transpose(0, 3, 2, 1)
    wgu = np.stack([tiles(f["L3_W_gate"]), tiles(f["L3_W_up"])], axis=1).reshape(2 * FT, P, LT * P)
    wd = np.pad(f["L3_W_down"], ((0, 0), (0, pad))).reshape(LT, P, FT, P).transpose(0, 3, 2, 1)
    la = lambda a: a[0].reshape(16, R, LT, P).transpose(0, 3, 2, 1).reshape(16, P, LT * R)
    lad = np.pad(f["L3_A_down"][0], ((0, 0), (0, 0), (0, pad))).reshape(16, R, FT, P)
    lb = lambda b: np.pad(b[0], ((0, 0), (0, pad), (0, 0))).reshape(16, FT, P, R).transpose(0, 1, 3, 2)
    arrays = {
        "u": u,
        "urev": u[::-1],
        "params": np.concatenate([params, params]),
        "D": f["L0_D"].reshape(1, H),
        "length": f["itok_B_78_3631"].reshape(1, B),
        "ids": np.concatenate([f["itok_B_0_15"], f["itok_B_1_14"], f["itok_B_2_6"]]).reshape(1, 3 * B),
        "w1": picked(f["L1_weight"]),
        "w2": picked(f["L2_weight"]),
        "wgu": wgu,
        "wd0": wd[:, :, :F0].reshape(LT, P, F0 * P),
        "wd1": wd[:, :, F0:].reshape(LT, P, F1 * P),
        "lora_a": np.stack([la(f["L3_A_gate"]), la(f["L3_A_up"])], axis=1),
        "lora_ad": lad.transpose(0, 3, 2, 1).reshape(16, P, FT * R),
        "lora_b": np.stack([lb(f["L3_B_gate"]), lb(f["L3_B_up"])], axis=2).reshape(16, 2 * FT, R, P),
        "lora_bd": f["L3_B_down"][0].reshape(16, LT, P, R).transpose(0, 1, 3, 2),
    }
    arrays = {k: np.ascontiguousarray(v) for k, v in arrays.items()}
    nc = bacc.Bacc("TRN2", target_bir_lowering=False, num_devices=1)
    ins = {k: nc.dram_tensor("in_" + k, v.shape, mybir.dt.from_np(v.dtype), kind="ExternalInput").ap()
           for k, v in arrays.items()}
    out = nc.dram_tensor("y", [NTILE, P, TB, LT, H], F32, kind="ExternalOutput").ap()
    build(nc, ins, out)
    run = run_bass_kernel_spmd(nc, [{"in_" + k: v for k, v in arrays.items()}], core_ids=[0])
    y = run.results[0]["y"]
    return np.ascontiguousarray(y.transpose(0, 2, 4, 3, 1).reshape(B, H, L))
```

```python
import math
from contextlib import ExitStack

import concourse.bass as bass
from concourse import mybir

F32 = mybir.dt.float32
F32R = mybir.dt.float32r
I32 = mybir.dt.int32
ALU = mybir.AluOpType
ACT = mybir.ActivationFunctionType

P = 128
B, H, L = 32, 64, 1024
LT = L // P
ROWS = B * H
NS = 64
KB = 32
KPAD = P + L

CH = 8
NCHUNK = H // CH
AHEAD = 2
TG = 2
RING = 4
PAIRS = CH // TG
assert PAIRS == RING == 4

WC = 4
WK = LT // 2
WN = L // 2
NPICK = 16
STEPS = (B + NPICK) // 2
SPARE = 3
assert STEPS % 2 == 0 and STEPS <= B

FF = 2752
FT = -(-FF // P)
HALF = FF % P
F0 = 12
F1 = FT - F0
TILE = 512
NTILE = ROWS // TILE
TB = TILE // H
R = 16
NPAN = 2 + 2 * F0 + 1 + LT + 2 * F1 + 1 + LT
RAW = 4
PANB = 12
AD0 = 2 + 2 * F0
GU1 = AD0 + 1 + LT
AD1 = GU1 + 2 * F1
GATE = (0, 2)
DOWN = (4, 5, 7)
BANK_A, BANK_AD = 7, 6
GATHERED = TB * 5 * 16
TURN = 4
CHUNK_LINKS = 12
assert HALF == P // 2 and NPAN % RAW == 0 and F0 % 2 == 0 and F1 % 2 == 0

PI = float.fromhex("0x1.921fb4p+1")
TWO_PI = 2 * math.pi
TWO_PI_1 = 6.28125
TWO_PI_2 = TWO_PI - TWO_PI_1
LN2_1 = 0.693359375
LN2_2 = math.log(2) - LN2_1
MAGIC = 1.5 * 2 ** 23


def build(nc, ins, out):
    with ExitStack() as ctx:
        sem = lambda name: ctx.enter_context(nc.semaphore(name))

        def sb(stack, name, shape, dt=F32):
            return stack.enter_context(nc.sbuf_tensor(name, shape, dt))

        kpad = nc.dram_tensor("kpad", [H, KPAD], F32).ap()
        lora_a = nc.dram_tensor("picked_a", [NTILE, 2, P, TB, LT * R], F32).ap()
        lora_ad = nc.dram_tensor("picked_ad", [NTILE, P, TB, FT * R], F32).ap()
        lora_b = nc.dram_tensor("picked_b", [NTILE, 2 * FT, P, P], F32).ap()
        lora_bd = nc.dram_tensor("picked_bd", [NTILE, LT, P, P], F32).ap()

        X = sb(ctx, "X", [P, B + SPARE, LT, H])
        hid = [X[:, B + k].rearrange("p l h -> p (l h)") for k in range(2)]
        lora_mask = X[:, B + 2].rearrange("p l h -> p (l h)").rearrange("p (b h) -> p b h", h=H)

        region = nc.sbuf_base
        REGION = 100 * 1024

        early = ExitStack()
        table = sb(early, "table", [2, 3, STEPS], I32)
        turns = sb(early, "turns", [2, 1], I32)
        tick = sb(early, "tick", [1, 8])

        with ExitStack() as s:
            toep = sb(s, "toep", [P, RING, TG, L])
            u = sb(s, "u", [P, RING, TG, LT, B])
            urev = sb(s, "urev", [P, RING, TG, LT, B])
            par = sb(s, "par", [P, 5, H])
            drow = sb(s, "drow", [1, H])
            leni = sb(s, "leni", [P, B], I32)
            lenf = sb(s, "lenf", [P, B])
            lpos = sb(s, "lpos", [P, LT])
            lmask = sb(s, "lmask", [P, LT, B])
            kk = sb(s, "kk", [P, 2 * KB])
            quarter = sb(s, "quarter", [P, 4])
            ex = sb(s, "ex", [P, 12, H])
            exi = sb(s, "exi", [P, 2, H], I32)
            dta = sb(s, "dta", [P, 2, H])
            ct = sb(s, "ct", [P, 2, H])
            ang = sb(s, "ang", [P, CH, 2 * KB])
            turn = sb(s, "turn", [P, CH, 2 * KB])
            mag = sb(s, "mag", [P, CH, 2 * KB])
            red = sb(s, "red", [P, CH, 2 * KB])
            red2 = sb(s, "red2", [P, CH, KB])
            sin1 = sb(s, "sin1", [P, CH, 2 * KB])
            sin2 = sb(s, "sin2", [P, CH, KB])
            ge = sb(s, "ge", [P, CH, 2 * KB])
            ksb = sb(s, "ksb", [KB, CH, KB])
            zrow = sb(s, "zrow", [H, P])
            masked = sb(s, "masked", [P, 2, 2, LT, B])
            picki = sb(s, "picki", [2, B], I32)
            tri = sb(s, "tri", [2, B, B])
            seqs = sb(s, "seqs", [2, B])
            steps = sb(s, "steps", [2, STEPS])
            spare = sb(s, "spare", [2, 2, STEPS])
            pk = sb(s, "pk", [2, 6, B])
            pair = sb(s, "pair", [2, B, B])
            hit = [sb(s, f"hit{k}", [2, STEPS, B]) for k in range(2)]
            assert nc.sbuf_base <= region + REGION
            found = sb(s, "found", [2, 5, STEPS])

        with ExitStack() as s:
            ident = sb(s, "ident", [P, P])
            wh = sb(s, "wh", [P, WC, WK, WN], F32R)
            wl = sb(s, "wl", [P, WC, WK, WN], F32R)
            rh = sb(s, "rh", [P, 2, LT, 2 * H], F32R)
            rl = sb(s, "rl", [P, 2, LT, 2 * H], F32R)
            prod = sb(s, "prod", [2 * H, 2, L])
            sb(s, "gap", [P, (region + REGION - nc.sbuf_base) // 4])
            W = sb(s, "W", [P, WC, WK, WN])
        early.close()

        with ExitStack() as s:
            tmh = sb(s, "tmh", [P, 2, TILE], F32R)
            tml = sb(s, "tml", [P, 2, TILE], F32R)
            ph = sb(s, "ph", [P, 2, PANB * P], F32R)
            xh = sb(s, "xh", [P, LT, TILE], F32R)
            xl = sb(s, "xl", [P, LT, TILE], F32R)
            acth = sb(s, "acth", [P, F0, TILE], F32R)
            actl = sb(s, "actl", [P, F0, TILE], F32R)
            assert nc.sbuf_base == region + REGION
            raw = sb(s, "raw", [P, RAW, PANB * P])
            pl = sb(s, "pl", [P, 2, PANB * P], F32R)

        ps = ctx.enter_context(nc.psum_tensor("ps", [P, 8, 512], F32))

        par_in = sem("par_in")
        ids_in = sem("ids_in")
        consts = sem("consts")
        zero_set = sem("zero_set")
        zero_out = sem("zero_out")
        dve_link = sem("dve_link")
        half_arg = sem("half_arg")
        half_sin = sem("half_sin")
        u_in = [sem(f"u_in{i}") for i in range(RING)]
        toep_in = [sem(f"toep_in{i}") for i in range(RING)]
        mag_arg = sem("mag_arg")
        exp_done = sem("exp_done")
        sin_arg = sem("sin_arg")
        sin_done = sem("sin_done")
        ge_ready = sem("ge_ready")
        kmm_done = sem("kmm_done")
        k_copied = sem("k_copied")
        k_ready = sem("k_ready")
        k_out = sem("k_out")
        conv_done = sem("conv_done")
        conv_free = sem("conv_free")
        x1_done = sem("x1_done")
        w_in = [sem(f"w_in{i}") for i in range(WC)]
        table_ready = sem("table_ready")
        ident_set = sem("ident_set")
        mask_set = sem("mask_set")
        w_hi = sem("w_hi")
        w_lo = sem("w_lo")
        chunk_done = sem("chunk_done")
        rows_hi = sem("rows_hi")
        rows_cut = sem("rows_cut")
        prod_copied = sem("prod_copied")
        turned = sem("turned")
        step_added = sem("step_added")
        lora_out = sem("lora_out")
        raw_in = [sem(f"raw_in{i}") for i in range(RAW)]
        hi_ready = sem("hi_ready")
        lo_ready = sem("lo_ready")
        panel_done = sem("panel_done")
        rows_done = sem("rows_done")
        xh_ready = sem("xh_ready")
        xl_ready = sem("xl_ready")
        th_ready = sem("th_ready")
        t_ready = sem("t_ready")
        sig_ready = sem("sig_ready")
        silu_ready = sem("silu_ready")
        hid_ready = sem("hid_ready")
        act_ready = sem("act_ready")
        d_added = sem("d_added")
        y_out = sem("y_out")

        block = ctx.enter_context(nc.Block())
        KBANK = 6

        def bank(i):
            return ps[:, i, :]

        @block.sync
        def _(sp):
            sp.dma_start(par[:], ins["params"]).then_inc(par_in, 16)
            sp.dma_start(drow[:], ins["D"]).then_inc(par_in, 16)
            sp.dma_start(leni[:], ins["length"].to_broadcast([P, B])).then_inc(par_in, 16)
            sp.dma_start(picki[:], ins["ids"][:, 0:2 * B].rearrange("o (l b) -> (o l) b", l=2)
                         ).then_inc(ids_in, 16)
            sp.wait_ge(zero_set, 1)
            sp.dma_start(kpad[:, 0:P], zrow[:]).then_inc(zero_out, 16)

            def load_inputs(g, i):
                chans = bass.ds(g * TG, TG)
                sp.dma_start(urev[:, i], ins["urev"][:, chans]).then_inc(u_in[i], 16)
                sp.dma_start(u[:, i], ins["u"][:, chans]).then_inc(u_in[i], 16)

            def load_toeplitz(g, i):
                base = kpad[bass.ds(g * TG, TG), 1:1 + L]
                src = bass.AP(tensor=base.tensor, offset=base.offset, ap=[[1, P], [KPAD, TG], [1, L]])
                sp.dma_start(toep[:, i], src).then_inc(toep_in[i], 16)

            def reload(c, k):
                q = c * PAIRS + k
                sp.wait_ge(x1_done, q - (RING - 1))
                load_inputs(q, k % RING)
                sp.wait_ge(conv_done, q - (RING - 1))
                if k == PAIRS:
                    sp.wait_ge(k_out, c * 16 + 32)
                load_toeplitz(q, k % RING)

            for q in range(RING):
                load_inputs(q, q)
            sp.wait_ge(zero_out, 16)
            sp.wait_ge(k_out, 16)
            for q in range(RING):
                load_toeplitz(q, q)
            with sp.Fori(0, NCHUNK - 1) as c:
                for k in range(PAIRS):
                    reload(c, RING + k)
            for k in range(RING, PAIRS):
                reload(NCHUNK - 1, k)

            sp.wait_ge(table_ready, 1)
            before = 0
            for layer, w in enumerate((ins["w1"], ins["w2"])):
                count = sp.value_load(turns[layer:layer + 1, 0:1], min_val=B // 4, max_val=STEPS // 2)
                with sp.Fori(0, count) as it:
                    for half in range(2):
                        pick = sp.value_load(table[layer:layer + 1, 0, bass.ds(it * 2 + half, 1)],
                                             min_val=0, max_val=NPICK - 1)
                        for c in range(WC):
                            sp.wait_ge(w_lo, (it * 2 + (before + half)) * WC + (c + 1))
                            sp.dma_start(W[:, c], w[bass.ds(pick, 1), c].rearrange("a p i o -> (a p) i o")
                                         ).then_inc(w_in[c], 16)
                before = before + count * 2

            def load(n, src, at=0, incs=32):
                width = src.shape[-1]
                sp.dma_start(raw[:, n % RAW, at:at + width], src).then_inc(raw_in[n % RAW], incs)

            def room(count):
                sp.wait_ge(lo_ready, count + 1)

            def load_adapter(n, count, t, k):
                room(count)
                load(n, lora_a[bass.ds(t, 1), k].rearrange("t p b w -> (t p) (b w)"))

            def load_down_adapter(n, t, first, tiles):
                room(t * NPAN + n)
                sp.dma_start(raw[:, n % RAW, 0:TB * tiles * R].rearrange("p (b w) -> p b w", b=TB),
                             lora_ad[bass.ds(t, 1), :, :, first * R:(first + tiles) * R]
                             .rearrange("t p b w -> (t p) b w")).then_inc(raw_in[n % RAW], 32)

            def load_gate_up(n, t, j, pan):
                room(t * NPAN + j * 4 + n)
                load(n, ins["wgu"][bass.ds(pan, 1)].rearrange("a p w -> (a p) w"), incs=16)
                load(n, lora_b[bass.ds(t, 1), bass.ds(pan, 1)].rearrange("t a p w -> (t a p) w"),
                     at=LT * P, incs=16)

            def load_last_gate_up(t):
                room(t * NPAN + (AD1 - 2))
                load(AD1 - 2, ins["wlast"][0])
                room(t * NPAN + (AD1 - 1))
                load(AD1 - 1, ins["wlast"][1], incs=16)
                sp.dma_start(raw[:, (AD1 - 1) % RAW, LT // 2 * P:(LT // 2 + 2) * P].rearrange(
                    "p (a w) -> p a w", a=2),
                    lora_b[bass.ds(t, 1), 2 * FT - 2:2 * FT].rearrange("t a p w -> (t p) a w")
                ).then_inc(raw_in[(AD1 - 1) % RAW], 16)

            sp.wait_ge(w_lo, before * WC + WC)
            sp.wait_ge(lora_out, GATHERED)
            load_adapter(0, 0, 0, 0)
            load_adapter(1, 1, 0, 1)
            with sp.Fori(0, NTILE) as t:
                for k in range(2):
                    load_gate_up(2 + k, t, 0, k)
                with sp.Fori(0, F0 // 2 - 1) as j:
                    for k in range(4):
                        load_gate_up(4 + k, t, j, j * 4 + (2 + k))
                for k in range(2):
                    load_gate_up(AD0 - 2 + k, t, 0, 2 * F0 - 2 + k)
                load_down_adapter(AD0, t, 0, F0)
                for o in range(LT):
                    room(t * NPAN + (AD0 + 1 + o))
                    load(AD0 + 1 + o, ins["wd0"][o])
                for k in range(2):
                    load_gate_up(GU1 + k, t, 0, 2 * F0 + k)
                with sp.Fori(0, F1 // 2 - 1) as j:
                    for k in range(4):
                        load_gate_up(GU1 + 2 + k, t, j, j * 4 + (2 * F0 + 2 + k))
                load_last_gate_up(t)
                load_down_adapter(AD1, t, F0, F1)
                for o in range(LT):
                    room(t * NPAN + (AD1 + 1 + o))
                    load(AD1 + 1 + o, ins["wd1"][o], incs=16)
                    if o == LT - 1:
                        sp.wait_ge(lora_out, ((t + 1) % NTILE + 1) * GATHERED)
                    load(AD1 + 1 + o, lora_bd[bass.ds(t, 1), o].rearrange("t p w -> (t p) w"),
                         at=F1 * P, incs=16)
                for k in range(2):
                    load_adapter(NPAN + k, t * NPAN + (NPAN + k), (t + 1) % NTILE, k)

        @block.gpsimd
        def _(pool):
            pool.memset(zrow[:], 0.0).then_inc(zero_set, 1)
            pool.iota(kk[:, 0:KB], pattern=[[1, KB]], base=0, channel_multiplier=0,
                      allow_small_or_imprecise_dtypes=True).then_inc(consts, 1)
            pool.iota(kk[:, KB:2 * KB], pattern=[[KB, KB]], base=0, channel_multiplier=0,
                      allow_small_or_imprecise_dtypes=True).then_inc(consts, 1)
            pool.iota(lpos[:], pattern=[[P, LT]], base=0, channel_multiplier=1,
                      allow_small_or_imprecise_dtypes=True).then_inc(consts, 1)
            for i, (upper, lower) in enumerate(((0.25, 0.0), (math.pi / 2, 0.0), (2.0, -2.0))):
                pool.wait_ge(consts, 3 + 2 * i)
                pool.memset(quarter[0:NS, i:i + 1], upper).then_inc(consts, 1)
                pool.wait_ge(consts, 4 + 2 * i)
                pool.memset(quarter[NS:P, i:i + 1], lower).then_inc(consts, 1)
            pool.wait_ge(consts, 9)
            pool.memset(tri[:], 1.0).then_inc(consts, 1)
            pool.iota(seqs[:], pattern=[[1, B]], base=0, channel_multiplier=0,
                      allow_small_or_imprecise_dtypes=True).then_inc(consts, 1)
            pool.iota(steps[:], pattern=[[1, STEPS]], base=0, channel_multiplier=0,
                      allow_small_or_imprecise_dtypes=True).then_inc(consts, 1)
            for k in range(2):
                pool.iota(spare[:, k].rearrange("l (t u) -> l t u", u=2), pattern=[[0, STEPS // 2], [k, 2]],
                          base=B + 2 * (1 - k), channel_multiplier=0,
                          allow_small_or_imprecise_dtypes=True).then_inc(consts, 1)
            pool.memset(X[:, B:B + SPARE], 0.0).then_inc(consts, 1)
            pool.wait_ge(consts, 15)
            pool.affine_select(out=tri[:], in_=tri[:], compare_op=ALU.is_ge, fill=0.0, base=-1,
                               pattern=[[1, B], [-1, B]], channel_multiplier=0).then_inc(consts, 1)

            def gather(t):
                tile = bass.ds(t, 1)
                for b in range(TB):
                    pick = pool.value_load(ins["ids"][0:1, bass.ds(t * TB + (2 * B + b), 1)],
                                           min_val=0, max_val=NPICK - 1)
                    one = bass.ds(pick, 1)
                    if b == 0 and not isinstance(t, int):
                        pool.wait_ge(d_added, t * (2 * LT) + (1 - 2 * LT))
                    for k in range(2):
                        pool.dma_start(lora_a[tile, k, :, b].rearrange("t p w -> (t p) w"),
                                       ins["lora_a"][one, k].rearrange("a p w -> (a p) w")).then_inc(lora_out, 16)
                    pool.dma_start(lora_ad[tile, :, b].rearrange("t p w -> (t p) w"),
                                   ins["lora_ad"][one].rearrange("a p w -> (a p) w")).then_inc(lora_out, 16)
                    pool.dma_start(lora_b[tile, :, b * R:(b + 1) * R].rearrange("t a r w -> (t a) (r w)"),
                                   ins["lora_b"][one].rearrange("a n r w -> (a n) (r w)")).then_inc(lora_out, 16)
                    pool.dma_start(lora_bd[tile, :, b * R:(b + 1) * R].rearrange("t a r w -> (t a) (r w)"),
                                   ins["lora_bd"][one].rearrange("a n r w -> (a n) (r w)")).then_inc(lora_out, 16)

            def store(t):
                for k in range(2):
                    pool.wait_ge(d_added, t * (2 * LT) + (LT + (k + 1) * LT // 2))
                    mine = slice(k * LT // 2, (k + 1) * LT // 2)
                    pool.dma_start(out[bass.ds(t, 1), :, :, mine].rearrange("t p b l h -> (t p) b l h"),
                                   X[:, bass.ds(t * TB, TB), mine]).then_inc(y_out, 16)

            gather(0)

            pool.wait_ge(step_added, 2)
            pool.memset(ident[:], 0.0).then_inc(ident_set, 1)
            pool.wait_ge(ident_set, 1)
            pool.affine_select(out=ident[:], in_=ident[:], compare_op=ALU.not_equal, fill=1.0, base=0,
                               pattern=[[-1, P]], channel_multiplier=1).then_inc(ident_set, 1)

            pool.wait_ge(rows_done, 1)
            pool.memset(lora_mask, 0.5).then_inc(mask_set, 1)
            pool.wait_ge(mask_set, 1)
            pool.affine_select(out=lora_mask, in_=lora_mask, compare_op=ALU.is_ge, fill=0.0, base=0,
                               pattern=[[-R, TB], [0, H]], channel_multiplier=1).then_inc(mask_set, 1)
            pool.wait_ge(mask_set, 2)
            pool.affine_select(out=lora_mask, in_=lora_mask, compare_op=ALU.is_ge, fill=0.0, base=R - 1,
                               pattern=[[R, TB], [0, H]], channel_multiplier=-1).then_inc(mask_set, 1)

            with pool.Fori(0, NTILE - 1) as t:
                gather(t + 1)
                store(t)
            store(NTILE - 1)
            pool.wait_ge(lora_out, NTILE * GATHERED)
            pool.wait_ge(y_out, 32 * NTILE)

        @block.scalar
        def _(act):
            act.wait_ge(half_arg, 1)
            nc.scalar.activation(ex[:, 8:10], ex[:, 8:10], ACT.Sin).then_inc(half_sin, 1)

            def sines(c):
                act.wait_ge(mag_arg, c + 1)
                nc.scalar.activation(mag[:], mag[:], ACT.Exp).then_inc(exp_done, 1)
                act.wait_ge(sin_arg, c + 1)
                nc.scalar.activation(sin1[:], red[:], ACT.Sin).then_inc(sin_done, 1)
                nc.scalar.activation(sin2[:], red2[:], ACT.Sin).then_inc(sin_done, 1)

            def kernel_out(c):
                act.wait_ge(kmm_done, c + 1)
                if not isinstance(c, int) or c > 0:
                    act.wait_ge(k_out, c * 16)
                nc.scalar.activation(ksb[:], ps[0:KB, KBANK, 0:CH * KB].rearrange("a (c b) -> a c b", c=CH),
                                     ACT.Copy).then_inc(k_copied, 1)
                act.wait_ge(k_ready, c + 1)
                dst = kpad[bass.ds(c * CH, CH), P:KPAD].rearrange("c (a b) -> a c b", a=KB)
                act.dma_start(dst, ksb[:]).then_inc(k_out, 16)

            sines(0)
            kernel_out(0)
            with act.Fori(1, NCHUNK) as c:
                sines(c)
                kernel_out(c)

            def cut_chunk(g, c):
                act.wait_ge(w_in[c], (g + 1) * 16)
                act.wait_ge(chunk_done, g * WC + (c + 1))
                nc.scalar.activation(wh[:, c], W[:, c], ACT.Copy).then_inc(w_hi, 1)

            def copy_product(g, half, o):
                act.wait_ge(chunk_done, g * WC + (2 * o + 2 + WC))
                nc.scalar.activation(prod[:, half, o * WN:(o + 1) * WN], bank(2 * half + o),
                                     ACT.Copy).then_inc(prod_copied, 1)

            def step_rows_hi(s, half, added):
                seqs = [act.value_load(table[layer:layer + 1, 1 + k, bass.ds(s, 1)],
                                       min_val=0, max_val=B + SPARE - 1) for k in range(2)]
                act.wait_ge(step_added, added)
                for k, seq in enumerate(seqs):
                    nc.scalar.activation(rh[:, half, :, k * H:(k + 1) * H],
                                         X[:, bass.ds(seq, 1)].rearrange("p a l h -> p (a l) h"),
                                         ACT.Copy).then_inc(rows_hi, 1)

            def picked_turn(it, base, first):
                for half in range(2):
                    s = it * 2 + half
                    g = base + s
                    lag = not (first and half == 0)
                    if lag:
                        cut_chunk(g, 0)
                        step_rows_hi(s, half, g + 1)
                        copy_product(g - 1, 1 - half, 0)
                    cut_chunk(g, 1)
                    if lag:
                        copy_product(g - 1, 1 - half, 1)
                    cut_chunk(g, 2)
                    cut_chunk(g, 3)

            act.wait_ge(table_ready, 1)
            base = 0
            for layer in range(2):
                count = act.value_load(turns[layer:layer + 1, 0:1], min_val=B // 4, max_val=STEPS // 2)
                step_rows_hi(0, 0, base + 2)
                if layer == 0:
                    cut_chunk(0, 0)
                picked_turn(0, base, True)
                with act.Fori(1, count) as it:
                    picked_turn(it, base, False)
                base = base + count * 2
                copy_product(base - 1, 1, 0)
                if layer == 0:
                    cut_chunk(base, 0)
                copy_product(base - 1, 1, 1)

            def come(n, t, j=0):
                act.wait_ge(raw_in[n % RAW], (t * (NPAN // RAW) + j + (n // RAW + 1)) * 32)
                act.wait_ge(panel_done, t * NPAN + j * 4 + (n + 1))

            def cut(n, blocks, t, j=0):
                come(n, t, j)
                nc.scalar.activation(ph[:, n % 2, 0:blocks * P], raw[:, n % RAW, 0:blocks * P],
                                     ACT.Copy).then_inc(hi_ready, 1)

            def cut_adapter(n, blocks, t):
                come(n, t)
                nc.scalar.activation(
                    ph[:, n % 2, 0:blocks * P].rearrange("p (k b r) -> p b k r", b=TB, r=R),
                    raw[:, n % RAW, 0:blocks * P].rearrange("p (b k r) -> p b k r", b=TB, r=R),
                    ACT.Copy).then_inc(hi_ready, 1)

            def cut_rows(t):
                for mine in (slice(0, LT // 2), slice(LT // 2, LT)):
                    nc.scalar.activation(xh[:, mine].rearrange("p l (b h) -> p b l h", h=H),
                                         X[:, bass.ds(t * TB, TB), mine], ACT.Copy).then_inc(xh_ready, 1)

            def sigmoid(pair, n, t, j=0):
                act.wait_ge(panel_done, t * NPAN + j * 4 + (n + 3))
                nc.scalar.activation(hid[pair % 2], bank(GATE[pair % 2]),
                                     ACT.Sigmoid).then_inc(sig_ready, 1)

            def sigmoid_last(t):
                act.wait_ge(panel_done, t * NPAN + (AD1 + 2))
                nc.scalar.activation(bank(GATE[1] + 1)[0:HALF], bank(GATE[1])[HALF:P], ACT.Copy)
                nc.scalar.activation(hid[1][0:HALF], bank(GATE[1])[0:HALF], ACT.Sigmoid).then_inc(sig_ready, 1)

            cut_adapter(0, LT, 0)
            cut_adapter(1, LT, 0)
            act.wait_ge(step_added, base + 2)
            cut_rows(0)
            with act.Fori(0, NTILE) as t:
                cut(2, LT + 1, t)
                cut(3, LT + 1, t)
                with act.Fori(0, F0 // 2 - 1) as j:
                    for k in range(2):
                        cut(4 + 2 * k, LT + 1, t, j)
                        cut(5 + 2 * k, LT + 1, t, j)
                        sigmoid(k, 3 + 2 * k, t, j)
                cut(AD0 - 2, LT + 1, t)
                cut(AD0 - 1, LT + 1, t)
                sigmoid(F0 - 2, AD0 - 3, t)
                cut_adapter(AD0, F0, t)
                cut(AD0 + 1, F0, t)
                sigmoid(F0 - 1, AD0 - 1, t)
                for o in range(1, LT):
                    cut(AD0 + 1 + o, F0, t)
                cut(GU1, LT + 1, t)
                cut(GU1 + 1, LT + 1, t)
                with act.Fori(0, F1 // 2 - 1) as j:
                    for k in range(2):
                        cut(GU1 + 2 + 2 * k, LT + 1, t, j)
                        cut(GU1 + 3 + 2 * k, LT + 1, t, j)
                        sigmoid(F0 + k, GU1 + 1 + 2 * k, t, j)
                cut(AD1 - 2, LT // 2, t)
                cut(AD1 - 1, LT // 2 + 2, t)
                sigmoid(FT - 2, AD1 - 3, t)
                cut_adapter(AD1, F1, t)
                cut(AD1 + 1, F1 + 1, t)
                sigmoid_last(t)
                cut(AD1 + 2, F1 + 1, t)
                cut_rows((t + 1) % NTILE)
                for o in range(2, LT):
                    cut(AD1 + 1 + o, F1 + 1, t)
                for k in range(2):
                    cut_adapter(NPAN + k, LT, t)

        @block.vector
        def _(dve):
            V = nc.vector
            linked = [0]

            def link(ins, before=0):
                linked[0] += 1
                ins.then_inc(dve_link, 1)
                dve.wait_ge(dve_link, before + linked[0])

            def round_turns(t, before=0):
                link(V.tensor_scalar_add(t, t, MAGIC), before)
                link(V.tensor_scalar_add(t, t, -MAGIC), before)

            def expm1_of(x, n, r, q, two):
                link(V.tensor_scalar(n, x, 1 / math.log(2), None, ALU.mult))
                round_turns(n)
                link(V.tensor_scalar(n, n, -126.0, 127.0, ALU.max, ALU.min))
                link(V.scalar_tensor_tensor(out=r, in0=n, scalar=-LN2_1, in1=x, op0=ALU.mult, op1=ALU.add))
                link(V.scalar_tensor_tensor(out=r, in0=n, scalar=-LN2_2, in1=r, op0=ALU.mult, op1=ALU.add))
                link(V.tensor_scalar(q, r, 1 / 40320, None, ALU.mult))
                for d in (5040, 720, 120, 24, 6, 2, 1):
                    link(V.scalar_tensor_tensor(out=q, in0=q, scalar=1 / d, in1=r, op0=ALU.add, op1=ALU.mult))
                link(V.tensor_scalar(two, n, 127.0, float(2 ** 23), ALU.add, ALU.mult))

            def tt(out_, a, b, op, before=0):
                link(V.tensor_tensor(out=out_, in0=a, in1=b, op=op), before)

            V.memset(tick[:, 0:1], 0.0).then_inc(conv_free, RING)
            V.memset(tick[:, 1:2], 0.0).then_inc(w_lo, WC)
            link(V.memset(ex[:], 0.0))
            dve.wait_ge(par_in, 48)
            dve.wait_ge(consts, 9)

            two = exi[:, 0:2].bitcast(F32)
            expm1_of(par[:, 0:2], ex[:, 0:2], ex[:, 2:4], ex[:, 4:6], exi[:, 0:2])
            tt(ex[:, 6:8], ex[:, 4:6], two, ALU.mult)
            tt(ex[:, 6:8], ex[:, 6:8], two, ALU.add)
            link(V.tensor_scalar(ex[:, 6], ex[:, 6], -1.0, None, ALU.mult))
            ar, dt, ai = ex[:, 6], ex[:, 7], par[:, 2]
            tt(dta[:, 0], ar, dt, ALU.mult)
            tt(dta[:, 1], ai, dt, ALU.mult)
            link(V.tensor_scalar(ex[:, 10:12], dta[:, 1:2].to_broadcast([P, 2, H]), 0.5, None, ALU.mult))
            link(V.tensor_scalar(ex[:, 4:6], ex[:, 10:12], 1 / TWO_PI, None, ALU.mult))
            link(V.tensor_scalar_add(ex[:, 5], ex[:, 5], 0.25))
            round_turns(ex[:, 4:6])
            for i, part in enumerate((TWO_PI_1, TWO_PI_2)):
                link(V.scalar_tensor_tensor(out=ex[:, 8:10], in0=ex[:, 4:6], scalar=-part,
                                            in1=ex[:, 10:12] if i == 0 else ex[:, 8:10],
                                            op0=ALU.mult, op1=ALU.add))
            link(V.tensor_scalar_add(ex[:, 9], ex[:, 9], math.pi / 2))
            V.tensor_scalar(ex[:, 8:10], ex[:, 8:10], PI, -PI, ALU.min, ALU.max).then_inc(half_arg, 1)
            def over_k(a, c, n):
                return a[:, bass.ds(c * CH, CH)].unsqueeze(2).to_broadcast([P, CH, n])

            all_k = kk[:].unsqueeze(1).to_broadcast([P, CH, 2 * KB])

            def phases(c, before=0):
                V.tensor_tensor(out=mag[:], in0=over_k(dta[:, 0], c, 2 * KB), in1=all_k,
                                op=ALU.mult).then_inc(mag_arg, 1)
                tt(ang[:], over_k(dta[:, 1], c, 2 * KB), all_k, ALU.mult, before)
                link(V.tensor_scalar(turn[:], ang[:], 1 / TWO_PI, quarter[:, 0:1], ALU.mult, ALU.add), before)
                round_turns(turn[:], before)
                for i, part in enumerate((TWO_PI_1, TWO_PI_2)):
                    link(V.scalar_tensor_tensor(out=red[:], in0=turn[:], scalar=-part,
                                                in1=ang[:] if i == 0 else red[:],
                                                op0=ALU.mult, op1=ALU.add), before)

            def quarter_turns(c, before=0):
                link(V.tensor_scalar(red[:], red[:], quarter[:, 1:2], PI, ALU.add, ALU.min), before)
                link(V.tensor_scalar(red[:], red[:], -PI, None, ALU.max), before)
                r = red[:, :, KB:2 * KB]
                link(V.tensor_scalar(turn[:, :, 0:KB], r, PI / 2, -TWO_PI, ALU.is_gt, ALU.mult), before)
                link(V.scalar_tensor_tensor(out=red2[:], in0=r, scalar=PI / 2, in1=turn[:, :, 0:KB],
                                            op0=ALU.add, op1=ALU.add), before)
                V.tensor_scalar(red2[:], red2[:], PI, -PI, ALU.min, ALU.max).then_inc(sin_arg, 1)

            def powers(c, before=0):
                dve.wait_ge(exp_done, c + 1)
                dve.wait_ge(sin_done, c * 2 + 2)
                if not isinstance(c, int) or c > 0:
                    dve.wait_ge(kmm_done, c)
                V.tensor_tensor(out=ge[:, :, 0:KB], in0=sin1[:, :, 0:KB], in1=mag[:, :, 0:KB], op=ALU.mult)
                V.tensor_tensor(out=sin1[:, :, KB:2 * KB], in0=sin1[:, :, KB:2 * KB],
                                in1=mag[:, :, KB:2 * KB], op=ALU.mult)
                tt(sin2[:], sin2[:], mag[:, :, KB:2 * KB], ALU.mult, before)
                V.tensor_tensor(out=sin1[:, :, KB:2 * KB], in0=sin1[:, :, KB:2 * KB],
                                in1=over_k(ct[:, 0], c, KB), op=ALU.mult)
                tt(sin2[:], sin2[:], over_k(ct[:, 1], c, KB), ALU.mult, before)
                V.tensor_tensor(out=ge[:, :, KB:2 * KB], in0=sin1[:, :, KB:2 * KB], in1=sin2[:],
                                op=ALU.add).then_inc(ge_ready, 1)

            def add_d(c):
                dve.wait_ge(k_copied, c + 1)
                V.tensor_tensor(out=ksb[0:1, :, 0:1], in0=ksb[0:1, :, 0:1],
                                in1=drow[0:1, bass.ds(c * CH, CH)].unsqueeze(2), op=ALU.add).then_inc(k_ready, 1)

            def add_conv(c, i):
                q = c * PAIRS + i
                dve.wait_ge(conv_done, q + 1)
                mi = masked[:, i % 2].rearrange("p e l b -> p e (l b)")
                V.tensor_tensor(out=mi, in0=bank(i % RING).rearrange("p (e w) -> p e w", e=2),
                                in1=lmask[:].rearrange("p l b -> p (l b)").unsqueeze(1)
                                .to_broadcast([P, 2, LT * B]), op=ALU.mult).then_inc(conv_free, 1)
                dve.wait_ge(conv_free, q + (RING + 1))
                V.tensor_tensor(out=X[:, 0:B].rearrange("p b l h -> p h l b")[:, bass.ds(c * CH + 2 * i, 2)],
                                in0=masked[:, i % 2], in1=u[:, i % RING],
                                op=ALU.add).then_inc(x1_done, 1)

            phases(0)
            quarter_turns(0)
            expm1_of(dta[:, 0], ex[:, 0], ex[:, 1], ex[:, 2], exi[:, 0])
            one = exi[:, 0].bitcast(F32)
            tt(ex[:, 2], ex[:, 2], one, ALU.mult)
            link(V.scalar_tensor_tensor(out=ex[:, 3], in0=one, scalar=-1.0, in1=ex[:, 2],
                                        op0=ALU.add, op1=ALU.add))
            dve.wait_ge(half_sin, 1)
            em, s2, c2, cr, ci = ex[:, 3], ex[:, 8], ex[:, 9], par[:, 3:4], par[:, 4:5]
            twice = lambda a: a.to_broadcast([P, 2, H])
            V.tensor_scalar_add(ex[:, 0], em, 1.0)
            V.tensor_tensor(out=ex[:, 4], in0=ar, in1=ar, op=ALU.mult)
            tt(ex[:, 5], ai, ai, ALU.mult)
            link(V.scalar_tensor_tensor(out=ex[:, 0], in0=ex[:, 0], scalar=-2.0, in1=s2,
                                        op0=ALU.mult, op1=ALU.mult))
            V.tensor_tensor(out=ex[:, 10], in0=ex[:, 4], in1=ex[:, 5], op=ALU.add)
            V.tensor_tensor(out=ex[:, 1], in0=ex[:, 0], in1=s2, op=ALU.mult)
            tt(ex[:, 2], ex[:, 0], c2, ALU.mult)
            V.reciprocal(ex[:, 10], ex[:, 10])
            tt(ex[:, 1], ex[:, 1], em, ALU.add)
            V.tensor_scalar(ex[:, 10], ex[:, 10], quarter[:, 2:3], None, ALU.mult)
            V.tensor_tensor(out=ex[:, 4:6], in0=twice(cr), in1=ex[:, 1:3], op=ALU.mult)
            tt(ex[:, 8:10], twice(ci), ex[:, 1:3], ALU.mult)
            V.tensor_tensor(out=ex[:, 0], in0=ex[:, 4], in1=ex[:, 9], op=ALU.add)
            tt(ex[:, 1], ex[:, 8], ex[:, 5], ALU.subtract)
            V.tensor_tensor(out=ex[:, 4:6], in0=twice(ex[:, 6:7]), in1=ex[:, 0:2], op=ALU.mult)
            tt(ex[:, 8:10], twice(par[:, 2:3]), ex[:, 0:2], ALU.mult)
            V.tensor_tensor(out=ex[:, 0], in0=ex[:, 4], in1=ex[:, 9], op=ALU.add)
            tt(ex[:, 1], ex[:, 5], ex[:, 8], ALU.subtract)
            tt(ct[:], ex[:, 0:2], twice(ex[:, 10:11]), ALU.mult)
            powers(0)
            add_d(0)
            for c in range(1, AHEAD):
                phases(c)
                quarter_turns(c)
                powers(c)
                add_d(c)
            link(V.tensor_copy(lenf[:], leni[:]))
            tt(lmask[:], lenf[:].unsqueeze(1).to_broadcast([P, LT, B]),
               lpos[:].unsqueeze(2).to_broadcast([P, LT, B]), ALU.is_gt)

            over_b = lambda a, n: a.unsqueeze(1).to_broadcast([2, n, B])
            of_b = lambda a: a.unsqueeze(2).to_broadcast([2, B, B])
            pick, rank, floor, odd, even, step = (pk[:, i] for i in range(6))

            def rank_sequences():
                dve.wait_ge(ids_in, 16)
                dve.wait_ge(consts, 16)
                link(V.tensor_copy(pick, picki[:]))
                tt(pair[:], of_b(pick), over_b(pick, B), ALU.is_equal)
                tt(pair[:], pair[:], tri[:], ALU.mult)
                link(V.reduce_sum(rank, pair[:], axis=mybir.AxisListType.X))
                link(V.tensor_scalar(floor, rank, 0.5, -0.25, ALU.mult, ALU.add))
                round_turns(floor)

            def number_steps():
                link(V.scalar_tensor_tensor(out=odd, in0=floor, scalar=-2.0, in1=rank, op0=ALU.mult, op1=ALU.add))
                link(V.tensor_scalar(even, odd, -1.0, 1.0, ALU.mult, ALU.add))
                tt(pair[:], of_b(pick), over_b(pick, B), ALU.is_gt)
                tt(pair[:], pair[:], over_b(even, B), ALU.mult)
                link(V.reduce_sum(step, pair[:], axis=mybir.AxisListType.X))
                tt(step, step, floor, ALU.add)

            def count_turns():
                link(V.reduce_max(found[:, 0, 0:1], step, axis=mybir.AxisListType.X))
                link(V.tensor_scalar(found[:, 0, 0:1], found[:, 0, 0:1], 0.5, 0.75, ALU.mult, ALU.add))
                round_turns(found[:, 0, 0:1])
                link(V.tensor_copy(turns[:], found[:, 0, 0:1]))
                tt(hit[1][:], over_b(step, STEPS), steps[:].unsqueeze(2).to_broadcast([2, STEPS, B]), ALU.is_equal)
                tt(hit[0][:], hit[1][:], over_b(even, STEPS), ALU.mult)
                tt(hit[1][:], hit[1][:], over_b(odd, STEPS), ALU.mult)

            def find_members():
                for k in range(2):
                    link(V.reduce_sum(found[:, k], hit[k][:], axis=mybir.AxisListType.X))
                tt(pair[:, 0:STEPS], hit[0][:], over_b(pick, STEPS), ALU.mult)
                link(V.reduce_sum(found[:, 2], pair[:, 0:STEPS], axis=mybir.AxisListType.X))

            def place_members():
                for k in range(2):
                    tt(hit[k][:], hit[k][:], over_b(seqs[:], STEPS), ALU.mult)
                    link(V.reduce_sum(found[:, 3 + k], hit[k][:], axis=mybir.AxisListType.X))
                link(V.tensor_scalar(found[:, 0:2], found[:, 0:2], -1.0, 1.0, ALU.mult, ALU.add))
                tt(found[:, 0:2], found[:, 0:2], spare[:], ALU.mult)
                tt(found[:, 3:5], found[:, 3:5], found[:, 0:2], ALU.add)
                V.tensor_copy(table[:], found[:, 2:5]).then_inc(table_ready, 1)

            rank_sequences()
            setup_links = linked[0]
            with dve.Fori(0, NCHUNK - AHEAD) as c:
                linked[0] = setup_links
                before = c * CHUNK_LINKS
                add_conv(c, 0)
                phases(c + AHEAD, before)
                add_conv(c, 1)
                quarter_turns(c + AHEAD, before)
                add_conv(c, 2)
                powers(c + AHEAD, before)
                add_conv(c, 3)
                add_d(c + AHEAD)
                assert linked[0] - setup_links == CHUNK_LINKS
            linked[0] = setup_links + (NCHUNK - AHEAD) * CHUNK_LINKS
            stages = [number_steps, count_turns, find_members, place_members]
            for c in range(NCHUNK - AHEAD, NCHUNK):
                for i in range(PAIRS):
                    add_conv(c, i)
                    if c == NCHUNK - AHEAD:
                        stages[i]()

            dve.wait_ge(x1_done, H // TG)
            V.memset(tick[:, 2:3], 0.0).then_inc(chunk_done, WC)
            V.memset(tick[:, 4:5], 0.0).then_inc(panel_done, 2)
            V.memset(tick[:, 5:6], 0.0).then_inc(lo_ready, RAW)
            V.memset(tick[:, 3:4], 0.0).then_inc(step_added, 2)

            def cut_chunk(g, c):
                dve.wait_ge(w_hi, g * WC + (c + 1))
                V.tensor_tensor(out=wl[:, c], in0=W[:, c], in1=wh[:, c].bitcast(F32),
                                op=ALU.subtract).then_inc(w_lo, 1)

            def place(s, k):
                return dve.value_load(table[layer:layer + 1, 1 + k, bass.ds(s, 1)],
                                      min_val=0, max_val=B + SPARE - 1)

            def step_rows_lo(s, g, half):
                for k in range(2):
                    seq = place(s, k)
                    dve.wait_ge(rows_hi, g * 2 + (k + 1))
                    mine = slice(k * H, (k + 1) * H)
                    V.tensor_tensor(out=rl[:, half, :, mine],
                                    in0=X[:, bass.ds(seq, 1)].rearrange("p a l h -> p (a l) h"),
                                    in1=rh[:, half, :, mine].bitcast(F32), op=ALU.subtract).then_inc(rows_cut, 1)

            def add_step(s, g):
                for k in range(2):
                    seq = place(s, k)
                    dve.wait_ge(turned, g + 1)
                    rows = X[:, bass.ds(seq, 1)].rearrange("p a l h -> p (a l) h")
                    ins_ = V.tensor_tensor(out=rows, in0=ps[:, TURN:TURN + 2].rearrange(
                        "p c (l w) -> p (c l) w", w=2 * H)[:, :, k * H:(k + 1) * H], in1=rows, op=ALU.add)
                ins_.then_inc(step_added, 1)

            dve.wait_ge(table_ready, 1)
            base = 0
            for layer in range(2):
                count = dve.value_load(turns[layer:layer + 1, 0:1], min_val=B // 4, max_val=STEPS // 2)
                step_rows_lo(0, base, 0)
                if layer == 0:
                    cut_chunk(0, 0)
                for half in range(2):
                    if half == 1:
                        cut_chunk(base + 1, 0)
                        step_rows_lo(1, base + 1, 1)
                    cut_chunk(base + half, 1)
                    cut_chunk(base + half, 2)
                    if half == 1:
                        add_step(0, base)
                    cut_chunk(base + half, 3)
                with dve.Fori(1, count) as it:
                    for half in range(2):
                        s = it * 2 + half
                        cut_chunk(base + s, 0)
                        step_rows_lo(s, base + s, half)
                        cut_chunk(base + s, 1)
                        cut_chunk(base + s, 2)
                        add_step(s - 1, base + s - 1)
                        cut_chunk(base + s, 3)
                base = base + count * 2
                if layer == 0:
                    cut_chunk(base, 0)
                add_step(count * 2 - 1, base - 1)
            dve.wait_ge(step_added, base + 2)
            V.memset(tick[:, 6:7], 0.0).then_inc(rows_done, 1)

            def cut(n, blocks, t, j=0):
                dve.wait_ge(hi_ready, t * NPAN + j * 4 + (n + 1))
                V.tensor_tensor(out=pl[:, n % 2, 0:blocks * P], in0=raw[:, n % RAW, 0:blocks * P],
                                in1=ph[:, n % 2, 0:blocks * P].bitcast(F32),
                                op=ALU.subtract).then_inc(lo_ready, 1)

            def cut_adapter(n, blocks, t):
                dve.wait_ge(hi_ready, t * NPAN + (n + 1))
                way = dict(b=TB, r=R)
                V.tensor_tensor(
                    out=pl[:, n % 2, 0:blocks * P].rearrange("p (k b r) -> p b k r", **way),
                    in0=raw[:, n % RAW, 0:blocks * P].rearrange("p (b k r) -> p b k r", **way),
                    in1=ph[:, n % 2, 0:blocks * P].bitcast(F32).rearrange("p (k b r) -> p b k r", **way),
                    op=ALU.subtract).then_inc(lo_ready, 1)

            def cut_rows(t, count):
                way = dict(h=H)
                for k in range(2):
                    dve.wait_ge(xh_ready, count * 2 + (k - 1))
                    mine = slice(k * LT // 2, (k + 1) * LT // 2)
                    V.tensor_tensor(out=xl[:, mine].rearrange("p l (b h) -> p b l h", **way),
                                    in0=X[:, bass.ds(t * TB, TB), mine],
                                    in1=xh[:, mine].bitcast(F32).rearrange("p l (b h) -> p b l h", **way),
                                    op=ALU.subtract).then_inc(xl_ready, 1)

            def adapter(k, count, n, bk, t):
                dve.wait_ge(panel_done, t * NPAN + (n + 3))
                mask, prod, part = lora_mask.rearrange("p b h -> p (b h)"), bank(bk), hid[count % 2]
                V.tensor_tensor(out=part, in0=prod, in1=mask, op=ALU.mult)
                V.tensor_tensor(out=tmh[:, k], in0=prod, in1=mask, op=ALU.mult).then_inc(th_ready, 1)
                dve.wait_ge(th_ready, t * 3 + (count + 1))
                V.tensor_tensor(out=tml[:, k], in0=part, in1=tmh[:, k].bitcast(F32),
                                op=ALU.subtract).then_inc(t_ready, 1)

            def hidden(pair, at, n, t, j=0, rows=P):
                count = t * FT + j * 2 + (pair + 1)
                part, gate, up = (a[0:rows] for a in (hid[pair % 2], bank(GATE[pair % 2]), bank(GATE[pair % 2] + 1)))
                dve.wait_ge(panel_done, t * NPAN + j * 4 + (n + 3))
                dve.wait_ge(sig_ready, count)
                V.tensor_tensor(out=part, in0=part, in1=gate, op=ALU.mult).then_inc(silu_ready, 1)
                dve.wait_ge(silu_ready, count)
                one = bass.ds(j * 2 + at, 1) if not isinstance(j, int) else slice(at, at + 1)
                hi, lo = (a[0:rows, one].rearrange("p a w -> p (a w)") for a in (acth, actl))
                V.tensor_tensor(out=hi, in0=part, in1=up, op=ALU.mult)
                V.tensor_tensor(out=part, in0=part, in1=up, op=ALU.mult).then_inc(hid_ready, 1)
                dve.wait_ge(hid_ready, count)
                V.tensor_tensor(out=lo, in0=part, in1=hi.bitcast(F32),
                                op=ALU.subtract).then_inc(act_ready, 1)

            def down(o, n, t):
                dve.wait_ge(panel_done, t * NPAN + (n + 3))
                rows = X[:, bass.ds(t * TB, TB), o]
                V.tensor_tensor(out=rows, in0=bank(DOWN[o % 3]).rearrange("p (b h) -> p b h", h=H), in1=rows,
                                op=ALU.add).then_inc(d_added, 1)

            cut_adapter(0, LT, 0)
            cut_adapter(1, LT, 0)
            cut_rows(0, 1)
            dve.wait_ge(mask_set, 3)
            with dve.Fori(0, NTILE) as t:
                cut(2, LT + 1, t)
                adapter(0, 0, 0, BANK_A, t)
                cut(3, LT + 1, t)
                adapter(1, 1, 1, BANK_AD, t)
                with dve.Fori(0, F0 // 2 - 1) as j:
                    for k in range(2):
                        cut(4 + 2 * k, LT + 1, t, j)
                        cut(5 + 2 * k, LT + 1, t, j)
                        hidden(k, k, 3 + 2 * k, t, j)
                cut(AD0 - 2, LT + 1, t)
                cut(AD0 - 1, LT + 1, t)
                hidden(F0 - 2, F0 - 2, AD0 - 3, t)
                cut_adapter(AD0, F0, t)
                cut(AD0 + 1, F0, t)
                hidden(F0 - 1, F0 - 1, AD0 - 1, t)
                cut(AD0 + 2, F0, t)
                for o in range(2, LT):
                    cut(AD0 + 1 + o, F0, t)
                    down(o - 2, AD0 - 1 + o, t)
                cut(GU1, LT + 1, t)
                down(LT - 2, GU1 - 2, t)
                cut(GU1 + 1, LT + 1, t)
                down(LT - 1, GU1 - 1, t)
                with dve.Fori(0, F1 // 2 - 1) as j:
                    for k in range(2):
                        cut(GU1 + 2 + 2 * k, LT + 1, t, j)
                        cut(GU1 + 3 + 2 * k, LT + 1, t, j)
                        hidden(F0 + k, k, GU1 + 1 + 2 * k, t, j)
                cut(AD1 - 2, LT // 2, t)
                cut(AD1 - 1, LT // 2 + 2, t)
                hidden(FT - 2, F1 - 2, AD1 - 3, t)
                cut_adapter(AD1, F1, t)
                cut(AD1 + 1, F1 + 1, t)
                hidden(FT - 1, F1 - 1, AD1 - 1, t, rows=HALF)
                cut(AD1 + 2, F1 + 1, t)
                adapter(0, 2, AD1, BANK_AD, t)
                cut_rows((t + 1) % NTILE, t + 2)
                for o in range(2, LT):
                    cut(AD1 + 1 + o, F1 + 1, t)
                    down(o - 2, AD1 - 1 + o, t)
                for k in range(2):
                    cut_adapter(NPAN + k, LT, t)
                    down(LT - 2 + k, NPAN - 2 + k, t)

        @block.tensor
        def _(pe):
            mm = nc.tensor.matmul

            def kernels(c):
                pe.wait_ge(ge_ready, c + 1)
                if not isinstance(c, int) or c > 0:
                    pe.wait_ge(k_copied, c)
                for h in range(CH):
                    last = mm(ps[0:KB, KBANK, h * KB:(h + 1) * KB], lhsT=ge[:, h, KB:2 * KB],
                              rhs=ge[:, h, 0:KB], start=True, stop=True)
                last.then_inc(kmm_done, 1)

            def convolve(c, i):
                pe.wait_ge(u_in[i % RING], (c * (PAIRS // RING) + (i // RING + 1)) * 32)
                pe.wait_ge(toep_in[i % RING], (c * (PAIRS // RING) + (i // RING + 1)) * 16)
                pe.wait_ge(conv_free, c * PAIRS + (i + 1))
                for e in range(TG):
                    rows = urev[:, i % RING, e].rearrange("p l b -> p (l b)")
                    for d in range(LT):
                        n = (LT - d) * B
                        last = mm(ps[:, i % RING, (e + 1) * LT * B - n:(e + 1) * LT * B],
                                  lhsT=toep[:, i % RING, e, d * P:(d + 1) * P], rhs=rows[:, 0:n],
                                  start=d == 0, stop=d == LT - 1)
                last.then_inc(conv_done, 1)

            for c in range(AHEAD):
                kernels(c)
            with pe.Fori(0, NCHUNK - AHEAD) as c:
                for i in range(PAIRS):
                    convolve(c, i)
                kernels(c + AHEAD)
            for c in range(NCHUNK - AHEAD, NCHUNK):
                for i in range(PAIRS):
                    convolve(c, i)

            def chunk(g, half, c):
                pe.wait_ge(w_lo, g * WC + (c + 1 + WC))
                to = bank(2 * half + c // 2)
                for k in range(WK):
                    at = (c % 2) * WK + k
                    first, end = at == 0, at == LT - 1
                    mm(to, lhsT=rh[:, half, at], rhs=wh[:, c, k], start=first, stop=False)
                    mm(to, lhsT=rh[:, half, at], rhs=wl[:, c, k], start=False, stop=False)
                    last = mm(to, lhsT=rl[:, half, at], rhs=wh[:, c, k], start=False, stop=end)
                last.then_inc(chunk_done, 1)

            def turn_product(g, half):
                pe.wait_ge(prod_copied, g * 2 + 2)
                pe.wait_ge(step_added, g + 2)
                for o in range(LT):
                    last = nc.tensor.transpose(ps[:, TURN + o // 4, (o % 4) * P:(o % 4 + 1) * P],
                                               prod[:, half, o * P:(o + 1) * P], ident[:])
                last.then_inc(turned, 1)

            def picked_turn(it, base, first):
                for half in range(2):
                    g = base + it * 2 + half
                    pe.wait_ge(rows_cut, g * 2 + 2)
                    chunk(g, half, 0)
                    if not (first and half == 0):
                        turn_product(g - 1, 1 - half)
                    chunk(g, half, 1)
                    chunk(g, half, 2)
                    chunk(g, half, 3)

            pe.wait_ge(ident_set, 2)
            pe.wait_ge(table_ready, 1)
            base = 0
            for layer in range(2):
                count = pe.value_load(turns[layer:layer + 1, 0:1], min_val=B // 4, max_val=STEPS // 2)
                picked_turn(0, base, True)
                with pe.Fori(1, count) as it:
                    picked_turn(it, base, False)
                base = base + count * 2
                turn_product(base - 1, 1)

            def panel(n, bk, blocks, hi, lo, t, j=0, start=True, stop=True, extra=(), extra_ready=0,
                      ready=None, sem=act_ready, at=0):
                pe.wait_ge(lo_ready, t * NPAN + j * 4 + (n + RAW + 1))
                moving = [(hi[:, at + k], lo[:, at + k]) for k in range(blocks)]
                moving += [(tmh[:, k], tml[:, k]) for k in extra]
                for k, (mh, ml) in enumerate(moving):
                    if extra and k == blocks:
                        pe.wait_ge(t_ready, t * 3 + extra_ready)
                    if ready and k in ready:
                        pe.wait_ge(sem, ready[k])
                    rows = HALF if hi is acth and n >= AD1 and k == F1 - 1 else P
                    wh, wl, mh, ml = (a[0:rows] for a in (ph[:, n % 2, k * P:(k + 1) * P],
                                                          pl[:, n % 2, k * P:(k + 1) * P], mh, ml))
                    first, end = start and k == 0, stop and k == len(moving) - 1
                    mm(bank(bk), lhsT=wh, rhs=mh, start=first, stop=False)
                    mm(bank(bk), lhsT=wh, rhs=ml, start=False, stop=False)
                    last = mm(bank(bk), lhsT=wl, rhs=mh, start=False, stop=end)
                last.then_inc(panel_done, 1)

            def gate_up(pair, n, t, j=0):
                for k in range(2):
                    panel(n + k, GATE[pair % 2] + k, LT, xh, xl, t, j,
                          extra=(k,), extra_ready=k + 1)

            with pe.Fori(0, NTILE) as t:
                panel(0, BANK_A, LT, xh, xl, t, ready={0: t * 2 + 1, LT // 2: t * 2 + 2}, sem=xl_ready)
                panel(1, BANK_AD, LT, xh, xl, t)
                with pe.Fori(0, F0 // 2) as j:
                    for k in range(2):
                        gate_up(k, 2 + 2 * k, t, j)
                done = lambda k: t * FT + (k + 1)
                panel(AD0, BANK_AD, F0, acth, actl, t, stop=False,
                      ready={0: done(F0 - 3), F0 - 2: done(F0 - 2), F0 - 1: done(F0 - 1)})
                for o in range(LT):
                    panel(AD0 + 1 + o, DOWN[o % 3], F0, acth, actl, t)
                with pe.Fori(0, F1 // 2 - 1) as j:
                    for k in range(2):
                        gate_up(k, GU1 + 2 * k, t, j)
                gate_up(0, AD1 - 4, t)
                panel(AD1 - 2, GATE[1], LT // 2, xh, xl, t, stop=False)
                panel(AD1 - 1, GATE[1], LT // 2, xh, xl, t, start=False, at=LT // 2,
                      extra=(0, 1), extra_ready=2)
                panel(AD1, BANK_AD, F1, acth, actl, t, start=False,
                      ready={0: done(FT - 3), F1 - 2: done(FT - 2), F1 - 1: done(FT - 1)})
                for o in range(LT):
                    panel(AD1 + 1 + o, DOWN[o % 3], F1, acth, actl, t,
                          extra=(0,), extra_ready=3)


def kernel(**inputs):
    import numpy as np
    import concourse.bacc as bacc
    from concourse.bass_utils import run_bass_kernel_spmd

    f = {k.replace("_cond", ""): np.asarray(v) for k, v in inputs.items()}

    u = f["x"].reshape(B, H, LT, P).transpose(3, 1, 2, 0)
    state = [f["L0_log_A_real"].T, np.broadcast_to(f["L0_log_dt"][None, :], (NS, H)), f["L0_A_imag"].T,
             f["L0_C"][:, :, 0].T, f["L0_C"][:, :, 1].T]
    params = np.stack(state, axis=1)
    picked = lambda w: w.reshape(NPICK, 2, WN, 2, WK, P).transpose(0, 1, 3, 5, 4, 2).reshape(
        NPICK, WC, P, WK, WN)
    pad = FT * P - FF
    tiles = lambda w: np.pad(w, ((0, pad), (0, 0))).reshape(FT, P, LT, P).transpose(0, 3, 2, 1)
    wgu = np.stack([tiles(f["L3_W_gate"]), tiles(f["L3_W_up"])], axis=1)
    last = np.concatenate([wgu[-1, 0, :, :, :HALF], wgu[-1, 1, :, :, :HALF]], axis=-1)
    wd = np.pad(f["L3_W_down"], ((0, 0), (0, pad))).reshape(LT, P, FT, P).transpose(0, 3, 2, 1)
    la = lambda a: a[0].reshape(16, R, LT, P).transpose(0, 3, 2, 1).reshape(16, P, LT * R)
    lad = np.pad(f["L3_A_down"][0], ((0, 0), (0, 0), (0, pad))).reshape(16, R, FT, P)
    lb = lambda b: np.pad(b[0], ((0, 0), (0, pad), (0, 0))).reshape(16, FT, P, R).transpose(0, 1, 3, 2)
    lora_b = np.stack([lb(f["L3_B_gate"]), lb(f["L3_B_up"])], axis=2)
    lora_b[:, -1, 1] = np.roll(lora_b[:, -1, 1], HALF, axis=-1)
    arrays = {
        "u": u,
        "urev": u[::-1],
        "params": np.concatenate([params, params]),
        "D": f["L0_D"].reshape(1, H),
        "length": f["itok_B_78_3631"].reshape(1, B),
        "ids": np.concatenate([f["itok_B_0_15"], f["itok_B_1_14"], f["itok_B_2_6"]]).reshape(1, 3 * B),
        "w1": picked(f["L1_weight"]),
        "w2": picked(f["L2_weight"]),
        "wgu": wgu[:-1].reshape(2 * FT - 2, P, LT * P),
        "wlast": last.reshape(P, 2, LT // 2 * P).transpose(1, 0, 2),
        "wd0": wd[:, :, :F0].reshape(LT, P, F0 * P),
        "wd1": wd[:, :, F0:].reshape(LT, P, F1 * P),
        "lora_a": np.stack([la(f["L3_A_gate"]), la(f["L3_A_up"])], axis=1),
        "lora_ad": lad.transpose(0, 3, 2, 1).reshape(16, P, FT * R),
        "lora_b": lora_b.reshape(16, 2 * FT, R, P),
        "lora_bd": f["L3_B_down"][0].reshape(16, LT, P, R).transpose(0, 1, 3, 2),
    }
    arrays = {k: np.ascontiguousarray(v) for k, v in arrays.items()}
    nc = bacc.Bacc("TRN2", target_bir_lowering=False, num_devices=1)
    ins = {k: nc.dram_tensor("in_" + k, v.shape, mybir.dt.from_np(v.dtype), kind="ExternalInput").ap()
           for k, v in arrays.items()}
    out = nc.dram_tensor("y", [NTILE, P, TB, LT, H], F32, kind="ExternalOutput").ap()
    build(nc, ins, out)
    run = run_bass_kernel_spmd(nc, [{"in_" + k: v for k, v in arrays.items()}], core_ids=[0])
    y = run.results[0]["y"]
    return np.ascontiguousarray(y.transpose(0, 2, 4, 3, 1).reshape(B, H, L))
```
